# Optimizing a Trainium2 kernel written in Bass

```python
import numpy as np
import jax
import jax.numpy as jnp

def _softmax(x, axis=-1):
    return jax.nn.softmax(x, axis=axis)

def _gelu(x):
    return jax.nn.gelu(x, approximate=True)

def _silu(x):
    return jax.nn.silu(x)

def _sigmoid(x):
    return jax.nn.sigmoid(x)

def _layernorm(x, axis=-1, eps=1e-05):
    m = jnp.mean(x, axis=axis, keepdims=True)
    v = jnp.var(x, axis=axis, keepdims=True)
    return (x - m) / jnp.sqrt(v + eps)

def _scatter_add(tgt, idx, src, axis=0):
    return tgt.at[idx].add(src)

def _segment_sum(src, seg, n):
    return jax.ops.segment_sum(src, seg, n)
kernel_name = 'mk_vit_tower_postln_d1_tok_img1024_r4_de017f'

def setup_inputs(seed: int=0):
    np.random.seed(seed)
    _w = jnp.asarray

    def _rec_inputs():
        import jax
        import jax.numpy as jnp
        _rk = jax.random.key(seed)
        x = -0.000222058 + 0.999998 * jax.random.normal(jax.random.fold_in(_rk, 1), (32, 3, 64, 64), jnp.float32)
        return x
    x = _rec_inputs()

    def _L0_tok_setup():
        import jax, jax.numpy as jnp
        import numpy as np
        IMG, PS, C, OUT = (64, 16, 3, 256)
        NP = IMG // PS
        IN_FEAT = C * PS * PS
        key = jax.random.key(seed)
        k1, k2, k3, k4 = jax.random.split(key, 4)
        x = jax.random.normal(k1, (128, C, IMG, IMG), dtype=jnp.float32)
        W = jax.random.normal(k2, (OUT, IN_FEAT), dtype=jnp.float32) / np.sqrt(IN_FEAT)
        b = jax.random.normal(k3, (OUT,), dtype=jnp.float32) * 0.01
        pos_emb = jax.random.normal(k4, (NP * NP, OUT), dtype=jnp.float32)
        return {'x': x, 'W': W, 'b': b, 'pos_emb': pos_emb}
    _L0_tok_all = _L0_tok_setup()
    _L0_tok_in = {k: v for k, v in _L0_tok_all.items() if k in ('W', 'b', 'pos_emb')}
    del _L0_tok_all

    def _L0_attn_setup():
        import jax, jax.numpy as jnp
        import numpy as np
        B, T, H = (32, 128, 256)
        L = 128
        E = 512
        S = 128
        SQRT_S = float(np.sqrt(S))
        EPS = 1e-05

        def _rope(x):
            half = x.shape[-1] // 2
            pos = jnp.arange(x.shape[1], dtype=x.dtype)
            inv_freq = 10000.0 ** (jnp.arange(half, dtype=x.dtype) / half)
            sinusoid = pos[:, None] * inv_freq[None, :]
            sin = jnp.sin(sinusoid)[None, :, None, :]
            cos = jnp.cos(sinusoid)[None, :, None, :]
            x1, x2 = jnp.split(x, 2, axis=-1)
            return jnp.concatenate([x1 * cos - x2 * sin, x2 * cos + x1 * sin], axis=-1)
        key = jax.random.key(seed)
        ks = jax.random.split(key, 9)
        return {'x': jax.random.normal(ks[0], (B, T, H), jnp.float32), 'ln_w': jnp.ones((H,), jnp.float32), 'ln_b': jnp.zeros((H,), jnp.float32), 'uv_w': jax.random.normal(ks[1], (2 * E + S, H), jnp.float32) * 0.02, 'uv_b': jnp.zeros((2 * E + S,), jnp.float32), 'gamma': jax.random.uniform(ks[2], (2, S), jnp.float32), 'beta': jax.random.uniform(ks[3], (2, S), jnp.float32), 'w': jax.random.uniform(ks[4], (2 * L - 1,), jnp.float32), 'o_w': jax.random.normal(ks[5], (H, E), jnp.float32) * 0.02, 'o_b': jnp.zeros((H,), jnp.float32)}
    _L0_attn_all = _L0_attn_setup()
    _L0_attn_in = {k: v for k, v in _L0_attn_all.items() if k in ('ln_w', 'ln_b', 'uv_w', 'uv_b', 'gamma', 'beta', 'w', 'o_w', 'o_b')}
    del _L0_attn_all

    def _L0_ffn_setup():
        import jax, jax.numpy as jnp
        import numpy as np
        B, S, H, E, DFF = (4, 1024, 256, 8, 1024)
        key = jax.random.key(seed)
        k0, k1, k2, k3 = jax.random.split(key, 4)
        hidden_states = jax.random.normal(k0, (B, S, H), dtype=jnp.float32)
        gate_w = jax.random.normal(k1, (E, H), dtype=jnp.float32) * 0.02
        w1 = jax.random.normal(k2, (E, H, DFF), dtype=jnp.float32) * 0.02
        b1 = jnp.zeros((E, DFF), dtype=jnp.float32)
        w2 = jax.random.normal(k3, (E, DFF, H), dtype=jnp.float32) * 0.02
        b2 = jnp.zeros((E, H), dtype=jnp.float32)
        return {'hidden_states': hidden_states, 'gate_w': gate_w, 'w1': w1, 'b1': b1, 'w2': w2, 'b2': b2}
    _L0_ffn_all = _L0_ffn_setup()
    _L0_ffn_in = {k: v for k, v in _L0_ffn_all.items() if k in ('gate_w', 'w1', 'b1', 'w2', 'b2')}
    del _L0_ffn_all
    return {'x': x, 'L0_tok_W': _L0_tok_in['W'], 'L0_tok_b': _L0_tok_in['b'], 'L0_tok_pos_emb': _L0_tok_in['pos_emb'], 'L0_attn_ln_w': _L0_attn_in['ln_w'], 'L0_attn_ln_b': _L0_attn_in['ln_b'], 'L0_attn_uv_w': _L0_attn_in['uv_w'], 'L0_attn_uv_b': _L0_attn_in['uv_b'], 'L0_attn_gamma': _L0_attn_in['gamma'], 'L0_attn_beta': _L0_attn_in['beta'], 'L0_attn_w': _L0_attn_in['w'], 'L0_attn_o_w': _L0_attn_in['o_w'], 'L0_attn_o_b': _L0_attn_in['o_b'], 'L0_ffn_gate_w': _L0_ffn_in['gate_w'], 'L0_ffn_w1': _L0_ffn_in['w1'], 'L0_ffn_b1': _L0_ffn_in['b1'], 'L0_ffn_w2': _L0_ffn_in['w2'], 'L0_ffn_b2': _L0_ffn_in['b2']}

def reference(x, L0_tok_W, L0_tok_b, L0_tok_pos_emb, L0_attn_ln_w, L0_attn_ln_b, L0_attn_uv_w, L0_attn_uv_b, L0_attn_gamma, L0_attn_beta, L0_attn_w, L0_attn_o_w, L0_attn_o_b, L0_ffn_gate_w, L0_ffn_w1, L0_ffn_b1, L0_ffn_w2, L0_ffn_b2):
    import jax
    import jax.numpy as jnp

    def _L0_tok_ref(x, W, b, pos_emb):
        import jax, jax.numpy as jnp
        import numpy as np
        IMG, PS, C, OUT = (64, 16, 3, 256)
        NP = IMG // PS
        IN_FEAT = C * PS * PS
        B = x.shape[0]
        p = x.reshape(B, C, NP, PS, NP, PS).transpose(0, 1, 2, 4, 3, 5)
        p = p.transpose(0, 2, 3, 1, 4, 5)
        p = p.reshape(B, NP * NP, IN_FEAT)
        out = jnp.einsum('bnf,of->bno', p, W) + b + pos_emb
        return out

    def _L0_attn_ref(x, ln_w, ln_b, uv_w, uv_b, gamma, beta, w, o_w, o_b):
        import jax, jax.numpy as jnp
        import numpy as np
        B, T, H = (32, 128, 256)
        L = 128
        E = 512
        S = 128
        SQRT_S = float(np.sqrt(S))
        EPS = 1e-05

        def _rope(x):
            half = x.shape[-1] // 2
            pos = jnp.arange(x.shape[1], dtype=x.dtype)
            inv_freq = 10000.0 ** (jnp.arange(half, dtype=x.dtype) / half)
            sinusoid = pos[:, None] * inv_freq[None, :]
            sin = jnp.sin(sinusoid)[None, :, None, :]
            cos = jnp.cos(sinusoid)[None, :, None, :]
            x1, x2 = jnp.split(x, 2, axis=-1)
            return jnp.concatenate([x1 * cos - x2 * sin, x2 * cos + x1 * sin], axis=-1)
        Tq = x.shape[1]
        shortcut = x
        mu = jnp.mean(x, axis=-1, keepdims=True)
        var = jnp.mean(jnp.square(x - mu), axis=-1, keepdims=True)
        xn = (x - mu) / jnp.sqrt(var + EPS) * ln_w + ln_b
        uv = jax.nn.silu(xn @ uv_w.T + uv_b)
        u, v, base = (uv[..., :E], uv[..., E:2 * E], uv[..., 2 * E:])
        base = base[:, :, None, :] * gamma[None, None] + beta
        base = _rope(base)
        q, k = (base[:, :, 0, :], base[:, :, 1, :])
        qk = jnp.einsum('bis,bjs->bij', q, k)
        rel = jnp.arange(Tq)[None, :] - jnp.arange(Tq)[:, None] + (L - 1)
        bias = w[rel]
        kernel = jnp.square(jax.nn.relu(qk / SQRT_S + bias[None]))
        out = u * jnp.einsum('bij,bje->bie', kernel, v)
        return out @ o_w.T + o_b + shortcut

    def _L0_ffn_ref(hidden_states, gate_w, w1, b1, w2, b2):
        import jax, jax.numpy as jnp
        import numpy as np
        B, S, H, E, DFF = (4, 1024, 256, 8, 1024)
        b, s, h = hidden_states.shape
        x = hidden_states.reshape(-1, h)
        gate_logits = x @ gate_w.T
        gate_probs = jax.nn.softmax(gate_logits, axis=-1)
        expert_idx = jnp.argmax(gate_probs, axis=-1)
        expert_w = jnp.take_along_axis(gate_probs, expert_idx[:, None], axis=1)[:, 0]
        out = jnp.zeros_like(x)
        n_experts = w1.shape[0]
        for e in range(n_experts):
            ye = jax.nn.relu(x @ w1[e] + b1[e]) @ w2[e] + b2[e]
            sel = (expert_idx == e)[:, None]
            out = out + jnp.where(sel, ye * expert_w[:, None], 0.0)
        return out.reshape(b, s, h)
    h = _L0_tok_ref(x, L0_tok_W, L0_tok_b, L0_tok_pos_emb)
    h = _layernorm(h + _L0_attn_ref(h, L0_attn_ln_w, L0_attn_ln_b, L0_attn_uv_w, L0_attn_uv_b, L0_attn_gamma, L0_attn_beta, L0_attn_w, L0_attn_o_w, L0_attn_o_b), axis=-1)
    h = _layernorm(h + _L0_ffn_ref(h, L0_ffn_gate_w, L0_ffn_w1, L0_ffn_b1, L0_ffn_w2, L0_ffn_b2), axis=-1)
    return h

_drawn_inputs = setup_inputs


def setup_inputs(seed=0):
    import zlib

    import numpy as np

    out = dict(_drawn_inputs(seed))
    spreads = {'L0_attn_ln_w': (1.0, 0.6),
     'L0_attn_ln_b': (0.0, 0.8),
     'L0_attn_uv_b': (0.0, 0.323),
     'L0_attn_o_b': (0.0, 0.8),
     'L0_ffn_b1': (0.0, 0.8),
     'L0_ffn_b2': (0.0, 0.407)}
    factors = {'L0_tok_b': 7.069, 'L0_attn_gamma': 23.673, 'L0_attn_beta': 8.0, 'L0_attn_w': 53.33}
    for name, (base, spread) in spreads.items():
        noise = np.random.default_rng([zlib.crc32(name.encode()), seed]).standard_normal(out[name].shape)
        drawn = base * np.exp(spread * noise) if base else spread * noise
        out[name] = jnp.asarray(drawn.astype(out[name].dtype))
    for name, factor in factors.items():
        out[name] = (out[name] * factor).astype(out[name].dtype)
    return out
```

```python
from contextlib import ExitStack

import numpy as np

import concourse.bass as bass
from concourse import mybir

ALU = mybir.AluOpType
ACT = mybir.ActivationFunctionType
F32 = mybir.dt.float32
BF16 = mybir.dt.bfloat16
I32 = mybir.dt.int32
U32 = mybir.dt.uint32
AX_X = mybir.AxisListType.X

P = 128
IMAGES, TOK, PATCH, CH, SIDE = 32, 16, 16, 3, 4
N = IMAGES * TOK
TILES = N // P
FEAT = CH * PATCH * PATCH
FK = FEAT // P
H = 256
HK = H // P
E_DIM = 512
EK = E_DIM // P
S = 128
UV = 2 * E_DIM + S
EXP = 8
DFF = 1024
DK = DFF // P
BIAS_LEN = 128
EPS = 1e-5
CHUNK = 128
MORE = sum(1 for c in range(1, N) if c * CHUNK + 1 <= N)
MAXC = N // CHUNK - 1
WCOLS = HK * DFF + DK * H

COLS = {}
_at = 0
for _name, _n in (("ln_w", HK), ("ln_b", HK), ("u_b", EK), ("base_b", 1), ("base_b_sw", 1), ("gamma", 2), ("beta", 2),
                  ("gamma_sw", 2), ("beta_sw", 2), ("b1", EXP * DK)):
    COLS[_name] = (_at, _n)
    _at += _n
NCOLS = _at
CONSTS = {}
_at = 0
for _name, _n in (("ident", P), ("block", P), ("cos", TOK), ("sin", TOK), ("rev", EXP), ("thr", EXP * MAXC),
                  ("expert", EXP * MAXC), ("nth", MORE * EXP * MAXC)):
    CONSTS[_name] = (_at, _n)
    _at += _n
NCONSTS = _at


def constant_table():
    t = np.zeros((P, NCONSTS), np.float32)

    def put(name, value):
        a, n = CONSTS[name]
        t[:, a:a + n] = value

    put("ident", np.eye(P))
    i = np.arange(P)
    put("block", i[:, None] // TOK == i[None, :] // TOK)
    half = S // 2
    inv = (10000.0 ** (np.arange(half) / half)).astype(np.float32)
    angle = (np.arange(TOK, dtype=np.float32)[None, :] * inv[:, None]).astype(np.float32)
    put("cos", np.concatenate([np.cos(angle), np.cos(angle)]))
    put("sin", np.concatenate([-np.sin(angle), np.sin(angle)]))
    put("rev", (EXP - np.arange(EXP))[None, :])
    put("thr", np.tile(CHUNK * (1 + np.arange(MAXC)), EXP)[None, :])
    put("expert", np.repeat(np.arange(EXP), MAXC)[None, :])
    put("nth", np.repeat(1 + np.arange(MORE), EXP * MAXC)[None, :])
    return t


def build(nc, xT, wT, uvT, owT, gateT, expw, cols_d, rows_d, pos_d, biasT_d, b2_d, const_d, out):
    ctx = ExitStack()
    with ctx:
        def sb(name, shape, dt=F32):
            return ctx.enter_context(nc.sbuf_tensor(name, shape, dt))

        def sem(name):
            return ctx.enter_context(nc.semaphore(name))

        bank = [ctx.enter_context(nc.psum_tensor(f"bank{i}", [P, 512], F32)) for i in range(8)]
        sorted_out = nc.dram_tensor("sorted_out", [N + CHUNK, H], F32, kind="Internal")

        slots = sb("slots", [P, EXP, WCOLS])
        w_emb = slots[:, 6, 0:FK * H].rearrange("p (k n) -> p k n", k=FK)
        w_uv = slots[:, 6, FK * H:FK * H + HK * UV].rearrange("p (k n) -> p k n", k=HK)
        x_in = slots[:, 7, 0:FK * N].rearrange("p (k n) -> p k n", k=FK)
        w_o = slots[:, 7, FK * N:FK * N + EK * H].rearrange("p (k n) -> p k n", k=EK)

        def w1(slot):
            return slots[:, slot, 0:HK * DFF].rearrange("p (k n) -> p k n", k=HK)

        def w2(slot):
            return slots[:, slot, HK * DFF:WCOLS].rearrange("p (k n) -> p k n", k=DK)

        cols = sb("cols", [P, NCOLS])
        rows = sb("rows", [P, 2 * H + E_DIM])
        tok_b, o_b, v_b = rows[:, 0:H], rows[:, H:2 * H], rows[:, 2 * H:]
        pos = sb("pos", [P, H])
        rel_bias = sb("rel_bias", [P, P])
        gate = sb("gate", [P, HK, EXP])
        const = sb("const", [P, NCONSTS])

        def col(name, i=0, n=1):
            return cols[:, COLS[name][0] + i:COLS[name][0] + i + n]

        def con(name, rows_=P):
            a, n = CONSTS[name]
            return const[0:rows_, a:a + n]

        ident = con("ident")
        iota = sb("iota", [P, N])
        upper = sb("upper", [P, P], BF16)
        ones = sb("ones", [P, P], BF16)
        minus_half = sb("minus_half", [P, 1])

        h = sb("h", [P, TILES, H])
        z = sb("z", [P, TILES, H])
        xn = sb("xn", [P, TILES, H])
        xnT = sb("xnT", [P, HK, N])
        uT = sb("uT", [P, EK, N])
        v = sb("v", [P, TILES, E_DIM])
        rotary = sb("rotary", [P, 6, N])
        base = rotary[:, 0:2, :]
        qk = rotary[:, 2:4, :]
        qk_sw = rotary[:, 4:6, :]
        b2 = rotary[:, 0:4, :].rearrange("p a n -> p (a n)").rearrange("p (e h) -> p e h", e=EXP)
        yc = rotary[:, 4, :].rearrange("p (b h) -> p b h", b=2)
        att = sb("att", [P, TILES, P])
        h2 = sb("h2", [P, TILES, H])
        h2T = sb("h2T", [P, TILES, HK, P])
        xs = sb("xs", [P, HK, N + CHUNK])
        xc = sb("xc", [P, 2, HK, CHUNK])
        by_token = xn
        result = xnT[:, :, :].rearrange("p k n -> p (k n)").rearrange("p (t h) -> p t h", t=TILES)
        onehot = uT
        hid = v[:, :, :].rearrange("p t e -> p (t e)").rearrange("p (b k c) -> p b k c", b=2, k=DK)

        b1_more = sb("b1_more", [P, MORE, DK])
        b2_more = sb("b2_more", [P, MORE, H])
        stats = sb("stats", [P, 3, TILES, 6])
        mv = sb("mv", [P, 3, TILES, 2])
        vare = sb("vare", [P, 3, TILES])
        rstd = sb("rstd", [P, 3, TILES])
        logit = sb("logit", [P, TILES, EXP])
        top = sb("top", [P, TILES])
        ntop = sb("ntop", [P, TILES])
        expl = sb("expl", [P, TILES, EXP])
        expsum = sb("expsum", [P, TILES])
        weight = sb("weight", [P, TILES])
        cand = sb("cand", [P, TILES, EXP])
        first = sb("first", [P, TILES])
        chosen = sb("chosen", [P, TILES, EXP])
        chosen_b = sb("chosen_b", [P, TILES * EXP], BF16)
        cnt = sb("cnt", [P, EXP, TILES])
        incl = sb("incl", [P, EXP, TILES])
        excl = sb("excl", [P, EXP, TILES])
        zero32 = sb("zero32", [P, EXP * TILES])
        rank = sb("rank", [P, TILES, EXP])
        slot = sb("slot", [P, TILES])
        slot_u = sb("slot_u", [P, TILES], U32)
        total = sb("total", [1, EXP])
        over = sb("over", [1, EXP, MAXC])
        place = sb("place", [1, EXP * MAXC])
        from_a = sb("from_a", [1, EXP, MAXC])
        end = sb("end", [1, EXP])
        pick = sb("pick", [1, 2, MORE, EXP * MAXC])
        pick2 = sb("pick2", [1, 2, MORE, EXP * MAXC])
        meta_f = sb("meta_f", [1, 16])
        meta = sb("meta", [1, 16], I32)
        M_MORE, M_EXPERT, M_FROM = EXP, EXP + 1, EXP + 1 + MORE

        in_x = [sem(f"in_x{k}") for k in range(FK)]
        in_const = sem("in_const")
        in_cols = sem("in_cols")
        in_rows = sem("in_rows")
        in_uv = sem("in_uv")
        in_ow = sem("in_ow")
        in_gate = sem("in_gate")
        in_b2 = sem("in_b2")
        in_w = [sem(f"in_w{e}") for e in range(EXP)]
        made_const = sem("made_const")
        posb_ready = sem("posb_ready")
        emb_done = sem("emb_done")
        h_ready = sem("h_ready")
        z0_ready = sem("z0_ready")
        stats_done = sem("stats_done")
        mv_ready = sem("mv_ready")
        vare_ready = sem("vare_ready")
        rstd_ready = sem("rstd_ready")
        xn_ready = sem("xn_ready")
        xnT_done = sem("xnT_done")
        xnT_ready = sem("xnT_ready")
        v_done = sem("v_done")
        vpre_ready = sem("vpre_ready")
        v_ready = sem("v_ready")
        base_done = sem("base_done")
        base_ready = sem("base_ready")
        affine_ready = sem("affine_ready")
        rope_a = sem("rope_a")
        rope_b = sem("rope_b")
        qk_ready = sem("qk_ready")
        u_done = sem("u_done")
        u_ready = sem("u_ready")
        score_done = sem("score_done")
        biased = sem("biased")
        clipped = sem("clipped")
        att_ready = sem("att_ready")
        av_done = sem("av_done")
        gated = sem("gated")
        o_done = sem("o_done")
        z_ready = sem("z_ready")
        h2_ready = sem("h2_ready")
        h2T_done = sem("h2T_done")
        h2T_ready = sem("h2T_ready")
        logit_done = sem("logit_done")
        route = sem("route")
        ntop_ready = sem("ntop_ready")
        exp_ready = sem("exp_ready")
        chosen_ready = sem("chosen_ready")
        rank_done = sem("rank_done")
        slot_ready = sem("slot_ready")
        onehot_ready = sem("onehot_ready")
        meta_ready = sem("meta_ready")
        sort_done = sem("sort_done")
        xs_ready = sem("xs_ready")
        xc_ready = sem("xc_ready")
        hid_done = sem("hid_done")
        hid_ready_a = sem("hid_ready_a")
        hid_ready_d = sem("hid_ready_d")
        b_more = sem("b_more")
        yc_done = sem("yc_done")
        yc_ready = sem("yc_ready")
        stored = sem("stored")
        fetched = [sem(f"fetched{t}") for t in range(TILES)]
        mixed = sem("mixed")
        out_ready = sem("out_ready")
        out_stored = sem("out_stored")

        block = ctx.enter_context(nc.Block())

        def tile(t):
            return slice(t * P, (t + 1) * P)

        def emb_bank(t):
            return bank[(0, 1, 6, 7)[t]][:, 0:H]

        def xnT_bank(t):
            return bank[2 + t % 2][:, 0:H].rearrange("p (k n) -> p k n", k=HK)

        def v_bank(t):
            return bank[4 + t % 2][:, :]

        base_bank = bank[6]

        def u_bank(m):
            return bank[(7, 0, 1, 2)[m]][:, :]

        def score_bank(t):
            return bank[(3, 3, 6, 6)[t]][:, (t % 2) * P:(t % 2 + 1) * P]

        def av_bank(t):
            return bank[4 + t % 2][:, :]

        def o_bank(t):
            return bank[(0, 1, 7, 2)[t]][:, 0:H]

        def h2T_bank(t):
            return bank[(3, 6, 0, 1)[t]][:, 0:H].rearrange("p (k n) -> p k n", k=HK)

        logit_bank = bank[4][:, 0:TILES * EXP]
        rank_bank = bank[4][:, 64:64 + TILES * EXP]
        cnt_bank = bank[4][:, 128:128 + TILES * EXP]

        def sort_bank(m):
            return bank[5 + m][:, :]

        def hid_bank(n, half):
            return bank[(7, 0, 1, 2)[2 * (n % 2) + half]]

        def yc_bank(n):
            return bank[3 + n % 2][:, 0:H]

        @block.sync
        def _(sp):
            for k in range(FK):
                sp.dma_start(x_in[:, k, :], xT[:, k, :]).then_inc(in_x[k], 16)
            sp.dma_start(w_uv, uvT).then_inc(in_uv, 16)
            sp.dma_start(w_o, owT).then_inc(in_ow, 16)
            sp.wait_ge(in_gate, 16)
            sp.wait_ge(in_rows, 48)
            for e in range(6):
                sp.dma_start(slots[:, e, :], expw[e]).then_inc(in_w[e], 16)
            sp.wait_ge(u_done, EK)
            sp.dma_start(slots[:, 6, :], expw[6]).then_inc(in_w[6], 16)
            sp.wait_ge(score_done, TILES)
            sp.dma_start(rotary[:, 0:4, :].rearrange("p a n -> p (a n)"), b2_d.partition_broadcast(P)).then_inc(in_b2, 16)
            sp.wait_ge(o_done, TILES)
            sp.dma_start(slots[:, 7, :], expw[7]).then_inc(in_w[7], 16)

            sp.wait_ge(meta_ready, 1)
            more = sp.value_load(meta[0:1, M_MORE:M_MORE + 1], min_val=0, max_val=MORE)
            for m in range(MORE):
                with sp.If(more > m):
                    e = sp.value_load(meta[0:1, M_EXPERT + m:M_EXPERT + m + 1], min_val=0, max_val=EXP - 1)
                    sp.wait_ge(yc_done, m + 1)
                    sp.dma_start(slots[:, m, :], expw[bass.ds(e, 1)].rearrange("a p n -> (a p) n"))\
                        .then_inc(in_w[m], 16)
            for n in range(EXP):
                start = sp.value_load(meta[0:1, n:n + 1], min_val=0, max_val=N)
                sp.wait_ge(yc_ready, n + 1)
                if n:
                    sp.wait_ge(stored, 16 * n)
                sp.dma_start(sorted_out[bass.ds(start, CHUNK), :], yc[:, n % 2, :]).then_inc(stored, 16)
            for m in range(MORE):
                n = EXP + m
                with sp.If(more > m):
                    start = sp.value_load(meta[0:1, M_FROM + m:M_FROM + m + 1], min_val=0, max_val=N)
                    sp.wait_ge(yc_ready, n + 1)
                    sp.wait_ge(stored, 16 * n)
                    sp.dma_start(sorted_out[bass.ds(start, CHUNK), :], yc[:, n % 2, :]).then_inc(stored, 16)

            for t in range(TILES):
                sp.wait_ge(out_ready, t + 1)
                sp.dma_start(out[tile(t), :], result[:, t, :]).then_inc(out_stored, 16)
            sp.wait_ge(out_stored, 16 * TILES)

        @block.gpsimd
        def _(pool):
            pool.memset(ones[:, :], 1.0).then_inc(made_const, 1)
            pool.memset(minus_half[:, :], -0.5).then_inc(made_const, 1)
            pool.memset(zero32[:, :], 0.0).then_inc(made_const, 1)
            pool.memset(xs[:, :, N:], 0.0).then_inc(made_const, 1)
            pool.wait_ge(made_const, 4)
            pool.affine_select(out=upper[:, :], in_=ones[:, :], compare_op=ALU.is_gt, fill=0.0, base=0,
                               pattern=[[1, P]], channel_multiplier=-1).then_inc(made_const, 1)
            pool.iota(iota[:, :], [[1, N]], base=0, channel_multiplier=0,
                      allow_small_or_imprecise_dtypes=True).then_inc(made_const, 1)
            pool.wait_ge(in_rows, 48)
            pool.tensor_tensor(pos[:, :], pos[:, :], tok_b, ALU.add).then_inc(posb_ready, 1)

            def rsqrt(ln, t):
                i = TILES * ln + t
                pool.wait_ge(mv_ready, i + 1)
                pool.tensor_scalar(vare[:, ln, t:t + 1], mv[:, ln, t, 1:2], EPS, None, ALU.add).then_inc(vare_ready, 1)
                pool.wait_ge(vare_ready, i + 1)
                pool.tensor_tensor(rstd[:, ln, t:t + 1], vare[:, ln, t:t + 1], minus_half[:, :], ALU.pow)\
                    .then_inc(rstd_ready, 1)

            for t in range(TILES):
                rsqrt(0, t)
            for t in range(TILES):
                pool.wait_ge(h_ready, t + 1)
                pool.tensor_tensor(z[:, t, :], h[:, t, :], h[:, t, :], ALU.add).then_inc(z0_ready, 1)
                pool.wait_ge(z0_ready, 2 * t + 1)
                pool.tensor_tensor(z[:, t, :], z[:, t, :], o_b, ALU.add).then_inc(z0_ready, 1)
            for t in range(TILES):
                rsqrt(1, t)

            pool.wait_ge(meta_ready, 1)
            more = pool.value_load(meta[0:1, M_MORE:M_MORE + 1], min_val=0, max_val=MORE)
            pool.wait_ge(stored, 16 * EXP)
            for m in range(MORE):
                with pool.If(more > m):
                    pool.wait_ge(stored, 16 * (EXP + m + 1))
            for t in range(TILES):
                pool.indirect_dma_start(by_token[:, t, :], None, sorted_out[0:N, :],
                                        bass.IndirectOffsetOnAxis(ap=slot_u[:, t:t + 1], axis=0))\
                    .then_inc(fetched[t], 16)
            for t in range(TILES):
                rsqrt(2, t)

        @block.scalar
        def _(act):
            for k in range(FK):
                act.dma_start(w_emb[:, k, :], wT[:, k, :]).then_inc(in_x[k], 16)
            act.dma_start(const[:, :], const_d).then_inc(in_const, 16)
            act.dma_start(cols[:, :], cols_d).then_inc(in_cols, 16)
            act.dma_start(rows[:, :], rows_d.partition_broadcast(P)).then_inc(in_rows, 16)
            act.dma_start(pos[:, :], pos_d).then_inc(in_rows, 16)
            act.dma_start(rel_bias[:, :], biasT_d).then_inc(in_rows, 16)
            act.dma_start(gate[:, :, :], gateT).then_inc(in_gate, 16)

            act.wait_ge(in_cols, 16)
            def xnT_copy(t):
                act.wait_ge(xnT_done, t + 1)
                for m in range(HK):
                    act.activation(xnT[:, m, tile(t)], xnT_bank(t)[:, m, :], ACT.Identity,
                                   scale=col("ln_w", m), bias=col("ln_b", m)).then_inc(xnT_ready, 1)

            def v_silu(t):
                act.wait_ge(vpre_ready, t + 1)
                act.activation(v[:, t, :], v[:, t, :], ACT.Silu).then_inc(v_ready, 1)

            for t in range(TILES):
                xnT_copy(t)
                if t >= 2:
                    v_silu(t - 2)
            v_silu(2)
            act.wait_ge(base_done, 1)
            act.activation(base[:, 0, :], base_bank[:, :], ACT.Silu, bias=col("base_b")).then_inc(base_ready, 1)
            for a, b in ((0, S // 2), (S // 2, 0)):
                act.activation(base[b:b + S // 2, 1, :], base_bank[a:a + S // 2, :], ACT.Silu,
                               bias=cols[a:a + S // 2, COLS["base_b"][0]:COLS["base_b"][0] + 1]).then_inc(base_ready, 1)
            v_silu(3)
            act.wait_ge(base_ready, 3)
            for j in range(2):
                act.activation(qk[:, j, :], base[:, 0, :], ACT.Identity, scale=col("gamma", j), bias=col("beta", j))\
                    .then_inc(affine_ready, 1)
                act.activation(qk_sw[:, j, :], base[:, 1, :], ACT.Identity, scale=col("gamma_sw", j),
                               bias=col("beta_sw", j)).then_inc(affine_ready, 1)
            for m in range(EK):
                act.wait_ge(u_done, m + 1)
                act.activation(uT[:, m, :], u_bank(m), ACT.Silu, bias=col("u_b", m)).then_inc(u_ready, 1)
            for t in range(TILES):
                act.wait_ge(h2T_done, t + 1)
                act.activation(h2T[:, t, :, :], h2T_bank(t), ACT.Copy).then_inc(h2T_ready, 1)
            for t in range(TILES):
                act.wait_ge(ntop_ready, 1)
                act.activation(expl[:, t, :], logit[:, t, :], ACT.Exp, bias=ntop[:, t:t + 1],
                               accum_out=expsum[:, t:t + 1]).then_inc(exp_ready, 1)
            act.wait_ge(sort_done, 1)
            act.activation(xs[:, 0, 0:N], sort_bank(0), ACT.Copy).then_inc(xs_ready, 1)

            def hidden(n, b1_col):
                act.wait_ge(hid_done, 2 * n + 1)
                if n >= 2:
                    act.wait_ge(yc_done, n - 1)
                for c in range(DK // 2):
                    act.activation(hid[:, n % 2, c, :], hid_bank(n, 0)[:, c * CHUNK:(c + 1) * CHUNK], ACT.Relu,
                                   bias=b1_col(c)).then_inc(hid_ready_a, 1)

            for n in range(EXP):
                hidden(n, lambda c, n=n: col("b1", n * DK + c))
            act.wait_ge(meta_ready, 1)
            more = act.value_load(meta[0:1, M_MORE:M_MORE + 1], min_val=0, max_val=MORE)
            for m in range(MORE):
                with act.If(more > m):
                    act.wait_ge(xc_ready, EXP + m + 1)
                    hidden(EXP + m, lambda c, m=m: b1_more[:, m, c:c + 1])

        @block.tensor
        def _(pe):
            for k in range(FK):
                pe.wait_ge(in_x[k], 32)
                for t in range(TILES):
                    mm = pe.matmul(emb_bank(t), x_in[:, k, tile(t)], w_emb[:, k, :], start=(k == 0), stop=(k == FK - 1))
                    if k == FK - 1:
                        mm.then_inc(emb_done, 1)
            pe.wait_ge(in_const, 16)

            def turn_xn(t):
                pe.wait_ge(xn_ready, t + 1)
                if t >= 2:
                    pe.wait_ge(xnT_ready, HK * (t - 1))
                for m in range(HK):
                    tr = pe.transpose(xnT_bank(t)[:, m, :], xn[:, t, tile(m)], ident)
                tr.then_inc(xnT_done, 1)

            def v_product(t):
                pe.wait_ge(xnT_ready, HK * (t + 1))
                if t >= 2:
                    pe.wait_ge(vpre_ready, t - 1)
                for k in range(HK):
                    mm = pe.matmul(v_bank(t), xnT[:, k, tile(t)], w_uv[:, k, E_DIM:2 * E_DIM], start=(k == 0),
                                   stop=(k == HK - 1))
                mm.then_inc(v_done, 1)

            turn_xn(0)
            turn_xn(1)
            pe.wait_ge(in_uv, 16)
            v_product(0)
            turn_xn(2)
            v_product(1)
            turn_xn(3)
            v_product(2)
            v_product(3)
            for k in range(HK):
                mm = pe.matmul(base_bank[:, :], w_uv[:, k, 2 * E_DIM:UV], xnT[:, k, :], start=(k == 0),
                               stop=(k == HK - 1))
            mm.then_inc(base_done, 1)
            for m in range(EK):
                for k in range(HK):
                    mm = pe.matmul(u_bank(m), w_uv[:, k, m * P:(m + 1) * P], xnT[:, k, :], start=(k == 0),
                                   stop=(k == HK - 1))
                mm.then_inc(u_done, 1)
            pe.wait_ge(qk_ready, 2)
            for t in range(TILES):
                pe.matmul(score_bank(t), qk[:, 1, tile(t)], qk[:, 0, tile(t)], start=True, stop=True)\
                    .then_inc(score_done, 1)

            def attend(t):
                pe.wait_ge(att_ready, t + 1)
                pe.wait_ge(v_ready, TILES)
                if t >= 2:
                    pe.wait_ge(gated, t - 1)
                for m in range(EK):
                    mm = pe.matmul(av_bank(t)[:, tile(m)], v[:, t, tile(m)], att[:, t, :], start=True, stop=True)
                mm.then_inc(av_done, 1)

            def project(t):
                pe.wait_ge(gated, t + 1)
                pe.wait_ge(in_ow, 16)
                for m in range(EK):
                    mm = pe.matmul(o_bank(t), uT[:, m, tile(t)], w_o[:, m, :], start=(m == 0), stop=(m == EK - 1))
                mm.then_inc(o_done, 1)

            def turn_h2(t):
                pe.wait_ge(h2_ready, t + 1)
                for m in range(HK):
                    tr = pe.transpose(h2T_bank(t)[:, m, :], h2[:, t, tile(m)], ident)
                tr.then_inc(h2T_done, 1)

            def logits(t):
                pe.wait_ge(h2T_ready, t + 1)
                pe.wait_ge(in_gate, 16)
                for m in range(HK):
                    mm = pe.matmul(logit_bank[:, t * EXP:(t + 1) * EXP], h2T[:, t, m, :], gate[:, m, :],
                                   start=(m == 0), stop=(m == HK - 1))
                mm.then_inc(logit_done, 1)

            attend(0)
            attend(1)
            project(0)
            attend(2)
            project(1)
            attend(3)
            project(2)
            turn_h2(0)
            project(3)
            turn_h2(1)
            logits(0)
            turn_h2(2)
            logits(1)
            turn_h2(3)
            logits(2)
            logits(3)

            pe.wait_ge(chosen_ready, 1)
            pe.wait_ge(made_const, 6)
            pe.matmul(rank_bank, upper[:, :], chosen_b[:, :], start=True, stop=True)
            pe.matmul(cnt_bank, ones[:, :], chosen_b[:, :], start=True, stop=True).then_inc(rank_done, 1)

            for m in range(HK):
                for t in range(TILES):
                    if m == 0:
                        pe.wait_ge(onehot_ready, t + 1)
                    mm = pe.matmul(sort_bank(m), h2[:, t, tile(m)], onehot[:, t, :], start=(t == 0),
                                   stop=(t == TILES - 1))
                mm.then_inc(sort_done, 1)

            def hidden(n, slot_):
                pe.wait_ge(xc_ready, n + 1)
                if n >= 2:
                    pe.wait_ge(hid_ready_a, DK // 2 * (n - 1))
                    pe.wait_ge(hid_ready_d, DK // 2 * (n - 1))
                for c in range(DK):
                    for k in range(HK):
                        mm = pe.matmul(hid_bank(n, c // 4)[:, (c % 4) * CHUNK:(c % 4 + 1) * CHUNK],
                                       w1(slot_)[:, k, c * P:(c + 1) * P], xc[:, n % 2, k, :], start=(k == 0),
                                       stop=(k == HK - 1))
                    if c % 4 == 3:
                        mm.then_inc(hid_done, 1)

            def output(n, slot_):
                if n >= 2:
                    pe.wait_ge(yc_ready, n - 1)
                for c in range(DK):
                    if c % 4 == 0:
                        pe.wait_ge(hid_ready_d if c else hid_ready_a, DK // 2 * (n + 1))
                    mm = pe.matmul(yc_bank(n), hid[:, n % 2, c, :], w2(slot_)[:, c, :], start=(c == 0),
                                   stop=(c == DK - 1))
                mm.then_inc(yc_done, 1)

            for n in range(EXP):
                pe.wait_ge(in_w[n], 16)
                hidden(n, n)
                if n:
                    output(n - 1, n - 1)
            output(EXP - 1, EXP - 1)
            more = pe.value_load(meta[0:1, M_MORE:M_MORE + 1], min_val=0, max_val=MORE)
            for m in range(MORE):
                with pe.If(more > m):
                    pe.wait_ge(in_w[m], 32)
                    hidden(EXP + m, m)
                    output(EXP + m, m)

        @block.vector
        def _(dve):
            def moments(ln, t, src):
                i = TILES * ln + t
                dve.bn_stats(stats[:, ln, t, :], src).then_inc(stats_done, 1)
                dve.wait_ge(stats_done, i + 1)
                dve.bn_aggr(mv[:, ln, t, :], stats[:, ln, t, :]).then_inc(mv_ready, 1)

            def normalise(ln, t, dst, src, done):
                dve.wait_ge(mv_ready, TILES * ln + t + 1)
                dve.wait_ge(rstd_ready, TILES * ln + t + 1)
                dve.tensor_scalar(dst, src, mv[:, ln, t, 0:1], rstd[:, ln, t:t + 1], ALU.subtract, ALU.mult)\
                    .then_inc(done, 1)

            dve.wait_ge(posb_ready, 1)
            for t in range(TILES + 1):
                if t < TILES:
                    dve.wait_ge(emb_done, t + 1)
                    dve.tensor_tensor(h[:, t, :], emb_bank(t), pos[:, :], ALU.add).then_inc(h_ready, 1)
                    dve.wait_ge(h_ready, t + 1)
                    moments(0, t, h[:, t, :])
                if t:
                    normalise(0, t - 1, xn[:, t - 1, :], h[:, t - 1, :], xn_ready)
            for t in range(TILES):
                dve.wait_ge(v_done, t + 1)
                dve.tensor_tensor(v[:, t, :], v_bank(t), v_b, ALU.add).then_inc(vpre_ready, 1)

            def over_images(name):
                return con(name).unsqueeze(1).to_broadcast([P, IMAGES, TOK])

            def by_image(ap):
                return ap.rearrange("p (i t) -> p i t", i=IMAGES)

            dve.wait_ge(in_const, 16)
            for j in range(2):
                dve.wait_ge(affine_ready, 2 * j + 1)
                dve.tensor_tensor(by_image(qk[:, j, :]), by_image(qk[:, j, :]), over_images("cos"), ALU.mult)\
                    .then_inc(rope_a, 1)
                dve.wait_ge(affine_ready, 2 * j + 2)
                dve.tensor_tensor(by_image(qk_sw[:, j, :]), by_image(qk_sw[:, j, :]), over_images("sin"), ALU.mult)\
                    .then_inc(rope_b, 1)
                dve.wait_ge(rope_a, j + 1)
                dve.wait_ge(rope_b, j + 1)
                dve.tensor_tensor(qk[:, j, :], qk[:, j, :], qk_sw[:, j, :], ALU.add).then_inc(qk_ready, 1)

            for t in range(TILES):
                dve.wait_ge(score_done, 2 * (t // 2) + 2)
                dve.scalar_tensor_tensor(out=att[:, t, :], in0=score_bank(t), scalar=1.0 / float(np.sqrt(S)),
                                         in1=rel_bias[:, :], op0=ALU.mult, op1=ALU.add).then_inc(biased, 1)
                dve.wait_ge(biased, t + 1)
                dve.scalar_tensor_tensor(out=att[:, t, :], in0=att[:, t, :], scalar=0.0, in1=con("block"),
                                         op0=ALU.max, op1=ALU.mult).then_inc(clipped, 1)
                dve.wait_ge(clipped, t + 1)
                dve.tensor_tensor(att[:, t, :], att[:, t, :], att[:, t, :], ALU.mult).then_inc(att_ready, 1)

            def gate_u(t):
                dve.wait_ge(av_done, t + 1)
                dve.wait_ge(u_ready, EK)
                dve.tensor_tensor(uT[:, :, tile(t)], uT[:, :, tile(t)],
                                  av_bank(t).rearrange("p (m n) -> p m n", m=EK), ALU.mult).then_inc(gated, 1)

            def residual(t):
                dve.wait_ge(o_done, t + 1)
                dve.wait_ge(z0_ready, 2 * (t + 1))
                dve.tensor_tensor(z[:, t, :], z[:, t, :], o_bank(t), ALU.add).then_inc(z_ready, 1)
                dve.wait_ge(z_ready, t + 1)
                moments(1, t, z[:, t, :])

            gate_u(0)
            gate_u(1)
            residual(0)
            gate_u(2)
            normalise(1, 0, h2[:, 0, :], z[:, 0, :], h2_ready)
            residual(1)
            gate_u(3)
            normalise(1, 1, h2[:, 1, :], z[:, 1, :], h2_ready)
            residual(2)
            normalise(1, 2, h2[:, 2, :], z[:, 2, :], h2_ready)
            residual(3)
            normalise(1, 3, h2[:, 3, :], z[:, 3, :], h2_ready)

            step = [0]

            def then(ins):
                step[0] += 1
                ins.then_inc(route, 1)
                dve.wait_ge(route, step[0])

            def per_tile(ap):
                return ap.unsqueeze(2).to_broadcast([P, TILES, EXP])

            dve.wait_ge(logit_done, TILES)
            then(dve.tensor_copy(logit[:, :, :], logit_bank.rearrange("p (t e) -> p t e", t=TILES)))
            then(dve.tensor_reduce(top[:, :], logit[:, :, :], AX_X, ALU.max))
            then(dve.tensor_tensor(cand[:, :, :], logit[:, :, :], per_tile(top[:, :]), ALU.is_equal))
            rev = con("rev").unsqueeze(1).to_broadcast([P, TILES, EXP])
            then(dve.tensor_tensor(cand[:, :, :], cand[:, :, :], rev, ALU.mult))
            then(dve.tensor_reduce(first[:, :], cand[:, :, :], AX_X, ALU.max))
            then(dve.tensor_tensor(chosen[:, :, :], rev, per_tile(first[:, :]), ALU.is_equal))
            dve.tensor_copy(chosen_b[:, :].rearrange("p (t e) -> p t e", t=TILES), chosen[:, :, :])\
                .then_inc(chosen_ready, 1)
            dve.tensor_scalar(ntop[:, :], top[:, :], -1.0, None, ALU.mult).then_inc(ntop_ready, 1)
            dve.wait_ge(rank_done, 1)
            dve.wait_ge(made_const, 4)
            then(dve.tensor_copy(cnt[:, :, :], cnt_bank.rearrange("p (t e) -> p e t", t=TILES)))
            cnt_row = cnt[:, :, :].rearrange("p e t -> p (e t)")
            incl_row = incl[:, :, :].rearrange("p e t -> p (e t)")
            then(dve.tensor_tensor_scan(incl_row, cnt_row, zero32[:, :], 0.0, ALU.add, ALU.add))
            then(dve.tensor_tensor(excl[:, :, :], incl[:, :, :], cnt[:, :, :], ALU.subtract))
            then(dve.tensor_tensor(rank[:, :, :], rank_bank.rearrange("p (t e) -> p t e", t=TILES),
                                   excl[:, :, :].rearrange("p e t -> p t e"), ALU.add))
            then(dve.tensor_tensor(rank[:, :, :], rank[:, :, :], chosen[:, :, :], ALU.mult))
            then(dve.tensor_reduce(slot[:, :], rank[:, :, :], AX_X, ALU.add))
            dve.wait_ge(gated, TILES)
            dve.wait_ge(o_done, TILES)
            for t in range(TILES):
                dve.tensor_scalar(onehot[:, t, :], iota[:, :], slot[:, t:t + 1], None, ALU.is_equal)\
                    .then_inc(onehot_ready, 1)
            dve.tensor_copy(slot_u[:, :], slot[:, :]).then_inc(slot_ready, 1)

            by_expert = [1, EXP, MAXC]

            def spread(ap):
                return ap.unsqueeze(2).to_broadcast(by_expert)

            offs = excl[0:1, :, 0]
            thr = con("thr", 1).rearrange("p (e c) -> p e c", e=EXP)
            then(dve.tensor_tensor(end[:, :], incl[0:1, :, TILES - 1], incl[0:1, :, TILES - 1], ALU.max))
            then(dve.tensor_tensor(total[:, :], end[:, :], offs, ALU.subtract))
            then(dve.tensor_tensor(over[:, :, :], spread(total[:, :]), thr, ALU.is_gt))
            over_row = over[:, :, :].rearrange("p e c -> p (e c)")
            then(dve.tensor_tensor_scan(place[:, :], over_row, zero32[0:1, 0:EXP * MAXC], 0.0, ALU.add, ALU.add))
            then(dve.tensor_copy(meta_f[:, M_MORE:M_MORE + 1], place[:, EXP * MAXC - 1:EXP * MAXC]))
            then(dve.tensor_tensor(place[:, :], place[:, :], over_row, ALU.mult))
            then(dve.tensor_tensor(from_a[:, :, :], spread(offs), thr, ALU.add))
            then(dve.tensor_scalar(end[:, :], end[:, :], float(-CHUNK), None, ALU.add))
            then(dve.tensor_tensor(from_a[:, :, :], from_a[:, :, :], spread(end[:, :]), ALU.min))
            nth = con("nth", 1).rearrange("p (m i) -> p m i", m=MORE)

            def for_each(ap):
                return ap.unsqueeze(1).to_broadcast([1, MORE, EXP * MAXC])

            then(dve.tensor_tensor(pick[:, 0, :, :], for_each(place[:, :]), nth, ALU.is_equal))
            then(dve.tensor_tensor(pick2[:, 0, :, :], pick[:, 0, :, :], for_each(con("expert", 1)), ALU.mult))
            then(dve.tensor_tensor(pick2[:, 1, :, :], pick[:, 0, :, :],
                                   for_each(from_a[:, :, :].rearrange("p e c -> p (e c)")), ALU.mult))
            then(dve.tensor_reduce(meta_f[:, M_EXPERT:M_EXPERT + 2 * MORE],
                                   pick2[:, :, :, :].rearrange("p a m i -> p (a m) i"), AX_X, ALU.add))
            then(dve.tensor_copy(meta_f[:, 0:EXP], offs))
            dve.tensor_copy(meta[:, 0:EXP + 1 + 2 * MORE], meta_f[:, 0:EXP + 1 + 2 * MORE]).then_inc(meta_ready, 1)
            dve.wait_ge(exp_ready, TILES)
            then(dve.reciprocal(weight[:, :], expsum[:, :]))

            dve.wait_ge(sort_done, 2)
            dve.tensor_copy(xs[:, 1, 0:N], sort_bank(1)).then_inc(xs_ready, 1)
            dve.wait_ge(xs_ready, 2)
            dve.wait_ge(meta_ready, 1)

            def fetch_chunk(n, at):
                start = dve.value_load(meta[0:1, at:at + 1], min_val=0, max_val=N)
                if n >= 2:
                    dve.wait_ge(hid_done, 2 * (n - 1))
                dve.tensor_copy(xc[:, n % 2, :, :], xs[:, :, bass.ds(start, CHUNK)]).then_inc(xc_ready, 1)

            def hidden(n, b1_col):
                dve.wait_ge(hid_done, 2 * n + 2)
                if n >= 2:
                    dve.wait_ge(yc_done, n - 1)
                for c in range(DK // 2, DK):
                    dve.tensor_scalar(hid[:, n % 2, c, :], hid_bank(n, 1)[:, (c - 4) * CHUNK:(c - 3) * CHUNK],
                                      b1_col(c), 0.0, ALU.add, ALU.max).then_inc(hid_ready_d, 1)

            def output(n, b2_row):
                dve.wait_ge(yc_done, n + 1)
                if n >= 2:
                    dve.wait_ge(stored, 16 * (n - 1))
                dve.tensor_tensor(yc[:, n % 2, :], yc_bank(n), b2_row, ALU.add).then_inc(yc_ready, 1)

            dve.wait_ge(in_b2, 16)
            dve.wait_ge(in_cols, 16)
            fetch_chunk(0, 0)
            fetch_chunk(1, 1)
            for n in range(EXP):
                hidden(n, lambda c, n=n: col("b1", n * DK + c))
                if n + 2 < EXP:
                    fetch_chunk(n + 2, n + 2)
                if n:
                    output(n - 1, b2[:, n - 1, :])
            output(EXP - 1, b2[:, EXP - 1, :])
            more = dve.value_load(meta[0:1, M_MORE:M_MORE + 1], min_val=0, max_val=MORE)
            for m in range(MORE):
                n = EXP + m
                with dve.If(more > m):
                    e = dve.value_load(meta[0:1, M_EXPERT + m:M_EXPERT + m + 1], min_val=0, max_val=EXP - 1)
                    b1_all = col("b1", 0, EXP * DK).rearrange("p (e c) -> p e c", e=EXP)
                    dve.tensor_copy(b1_more[:, m:m + 1, :], b1_all[:, bass.ds(e, 1), :]).then_inc(b_more, 1)
                    dve.tensor_copy(b2_more[:, m:m + 1, :], b2[:, bass.ds(e, 1), :]).then_inc(b_more, 1)
                    dve.wait_ge(b_more, 2 * m + 2)
                    fetch_chunk(n, M_FROM + m)
                    hidden(n, lambda c, m=m: b1_more[:, m, c:c + 1])
                    output(n, b2_more[:, m, :])

            for t in range(TILES + 1):
                if t < TILES:
                    dve.wait_ge(fetched[t], 16)
                    dve.scalar_tensor_tensor(out=by_token[:, t, :], in0=by_token[:, t, :], scalar=weight[:, t:t + 1],
                                             in1=h2[:, t, :], op0=ALU.mult, op1=ALU.add).then_inc(mixed, 1)
                    dve.wait_ge(mixed, t + 1)
                    moments(2, t, by_token[:, t, :])
                if t:
                    normalise(2, t - 1, result[:, t - 1, :], by_token[:, t - 1, :], out_ready)


def kernel(x, L0_tok_W, L0_tok_b, L0_tok_pos_emb, L0_attn_ln_w, L0_attn_ln_b, L0_attn_uv_w, L0_attn_uv_b,
           L0_attn_gamma, L0_attn_beta, L0_attn_w, L0_attn_o_w, L0_attn_o_b, L0_ffn_gate_w, L0_ffn_w1, L0_ffn_b1,
           L0_ffn_w2, L0_ffn_b2):
    import concourse.bacc as bacc
    from concourse.bass_utils import run_bass_kernel_spmd

    def chunks(a):
        a = np.asarray(a)
        return np.ascontiguousarray(a.reshape(a.shape[0] // P, P, a.shape[1]).transpose(1, 0, 2))

    def column(a):
        return np.asarray(a).reshape(-1, P).T

    def swap(a):
        return np.concatenate([a[S // 2:], a[:S // 2]])

    patches = np.asarray(x).reshape(IMAGES, CH, SIDE, PATCH, SIDE, PATCH).transpose(0, 2, 4, 1, 3, 5).reshape(N, FEAT)
    uv_b = np.asarray(L0_attn_uv_b)
    gamma, beta = np.asarray(L0_attn_gamma).T, np.asarray(L0_attn_beta).T
    base_b = uv_b[2 * E_DIM:].reshape(S, 1)
    cols = {"ln_w": column(L0_attn_ln_w), "ln_b": column(L0_attn_ln_b), "u_b": column(uv_b[:E_DIM]),
            "base_b": base_b, "base_b_sw": swap(base_b), "gamma": gamma, "beta": beta, "gamma_sw": swap(gamma),
            "beta_sw": swap(beta), "b1": column(np.asarray(L0_ffn_b1).reshape(-1))}
    local = np.arange(P) % TOK
    w1 = np.asarray(L0_ffn_w1).reshape(EXP, HK, P, DFF).transpose(0, 2, 1, 3).reshape(EXP, P, HK * DFF)
    w2 = np.asarray(L0_ffn_w2).reshape(EXP, DK, P, H).transpose(0, 2, 1, 3).reshape(EXP, P, DK * H)
    arrays = {
        "patchesT": chunks(patches.T),
        "embed_wT": chunks(np.asarray(L0_tok_W).T),
        "uv_wT": chunks(np.asarray(L0_attn_uv_w).T),
        "o_wT": chunks(np.asarray(L0_attn_o_w).T),
        "gate_wT": chunks(np.asarray(L0_ffn_gate_w).T),
        "expert_w": np.concatenate([w1, w2], axis=2),
        "param_cols": np.concatenate([cols[name] for name in COLS], axis=1),
        "param_rows": np.concatenate([np.asarray(L0_tok_b), np.asarray(L0_attn_o_b), uv_b[E_DIM:2 * E_DIM]]),
        "pos_emb": np.tile(np.asarray(L0_tok_pos_emb), (P // TOK, 1)),
        "rel_bias": np.asarray(L0_attn_w)[local[:, None] - local[None, :] + BIAS_LEN - 1],
        "expert_b2": np.asarray(L0_ffn_b2).reshape(-1),
        "consts": constant_table(),
    }
    nc = bacc.Bacc("TRN2", target_bir_lowering=False, num_devices=1)
    arrays = {k: np.ascontiguousarray(a) for k, a in arrays.items()}
    ins = [nc.dram_tensor(f"{k}_d", a.shape, mybir.dt.from_np(a.dtype), kind="ExternalInput").ap() for k, a in arrays.items()]
    out = nc.dram_tensor("out", [N, H], F32, kind="ExternalOutput").ap()
    build(nc, *ins, out)
    r = run_bass_kernel_spmd(nc, [{f"{k}_d": a for k, a in arrays.items()}], core_ids=[0])
    return r.results[0]["out"].reshape(IMAGES, TOK, H)
```

```python
from contextlib import ExitStack

import numpy as np

import concourse.bass as bass
from concourse import mybir

ALU = mybir.AluOpType
ACT = mybir.ActivationFunctionType
F32 = mybir.dt.float32
F32R = mybir.dt.float32r
BF16 = mybir.dt.bfloat16
I32 = mybir.dt.int32
U32 = mybir.dt.uint32
AX_X = mybir.AxisListType.X

P = 128
IMAGES, TOK, PATCH, CH, SIDE = 32, 16, 16, 3, 4
N = IMAGES * TOK
TILES = N // P
FEAT = CH * PATCH * PATCH
FK = FEAT // P
H = 256
HK = H // P
E_DIM = 512
EK = E_DIM // P
S = 128
UV = 2 * E_DIM + S
EXP = 8
HALF = N // 2
DFF = 1024
DK = DFF // P
BIAS_LEN = 128
EPS = 1e-5
CHUNK = 128
MORE = sum(1 for c in range(1, N) if c * CHUNK + 1 <= N)
MAXC = N // CHUNK - 1
WARMUP = 9
WCOLS = HK * DFF + DK * H

COLS = {}
_at = 0
for _name, _n in (("ln_w", HK), ("ln_b", HK), ("u_b", EK), ("base_b", 1), ("base_b_sw", 1), ("gamma", 2), ("beta", 2),
                  ("gamma_sw", 2), ("beta_sw", 2), ("b1", EXP * DK)):
    COLS[_name] = (_at, _n)
    _at += _n
NCOLS = _at
CONSTS = {}
_at = 0
for _name, _n in (("ident", P), ("block", P), ("cos", TOK), ("sin", TOK), ("rev", EXP), ("token", TILES), ("sum_parts", 2), ("thr", EXP * MAXC),
                  ("expert", EXP * MAXC), ("nth", MORE * EXP * MAXC)):
    CONSTS[_name] = (_at, _n)
    _at += _n
NCONSTS = _at


def constant_table():
    t = np.zeros((P, NCONSTS), np.float32)

    def put(name, value):
        a, n = CONSTS[name]
        t[:, a:a + n] = value

    put("ident", np.eye(P))
    i = np.arange(P)
    put("block", i[:, None] // TOK == i[None, :] // TOK)
    half = S // 2
    inv = (10000.0 ** (np.arange(half) / half)).astype(np.float32)
    angle = (np.arange(TOK, dtype=np.float32)[None, :] * inv[:, None]).astype(np.float32)
    put("cos", np.concatenate([np.cos(angle), np.cos(angle)]))
    put("sin", np.concatenate([-np.sin(angle), np.sin(angle)]))
    put("rev", (EXP - np.arange(EXP))[None, :])
    put("token", i[:, None] + P * np.arange(TILES)[None, :])
    t[0:3, CONSTS["sum_parts"][0]:CONSTS["sum_parts"][0] + 2] = [[1, 0], [1, 0], [0, 1]]
    put("thr", np.tile(CHUNK * (1 + np.arange(MAXC)), EXP)[None, :])
    put("expert", np.repeat(np.arange(EXP), MAXC)[None, :])
    put("nth", np.repeat(1 + np.arange(MORE), EXP * MAXC)[None, :])
    return t


def build(nc, xT, wT, uvT, owT, gateT, expw, cols_d, rows_d, embed_rows_d, biasT_d, b2_d, const_d, out):
    ctx = ExitStack()
    with ctx:
        def sb(name, shape, dt=F32):
            return ctx.enter_context(nc.sbuf_tensor(name, shape, dt))

        def sem(name):
            return ctx.enter_context(nc.semaphore(name))

        bank = [ctx.enter_context(nc.psum_tensor(f"bank{i}", [P, 512], F32)) for i in range(8)]

        slots = sb("slots", [P, EXP, WCOLS])
        w_emb = slots[:, 6, 0:FK * H].rearrange("p (k n) -> p k n", k=FK)
        w_uv = slots[:, 6, FK * H:FK * H + HK * UV].rearrange("p (k n) -> p k n", k=HK)
        x_in = slots[:, 7, 0:FK * N].rearrange("p (k n) -> p k n", k=FK)
        w_o = slots[:, 7, FK * N:FK * N + EK * H].rearrange("p (k n) -> p k n", k=EK)

        def w1(slot):
            return slots[:, slot, 0:HK * DFF].rearrange("p (k n) -> p k n", k=HK)

        def w2(slot):
            return slots[:, slot, HK * DFF:WCOLS].rearrange("p (k n) -> p k n", k=DK)

        cols = sb("cols", [P, NCOLS])
        embed_rows = sb("embed_rows", [TOK + 1, H + P])
        pos_and_b, token_pos = embed_rows[:, 0:H], embed_rows[:, H:]
        rows = sb("rows", [P, H + E_DIM])
        o_b, v_b = rows[:, 0:H], rows[:, H:]
        slot_rows = rows[0:3, 0:N + CHUNK]
        rel_bias = sb("rel_bias", [P, P])
        gate = sb("gate", [P, HK, EXP])
        const = sb("const", [P, NCONSTS])

        def col(name, i=0, n=1):
            return cols[:, COLS[name][0] + i:COLS[name][0] + i + n]

        def con(name, rows_=P):
            a, n = CONSTS[name]
            return const[0:rows_, a:a + n]

        ident = con("ident")
        iota = sb("iota", [P, N])
        upper = sb("upper", [P, P], BF16)
        ones = sb("ones", [P, P], BF16)
        minus_half = sb("minus_half", [P, 1])
        warm = sb("warm", [P, 1])

        xs = sb("xs", [P, HK, N + CHUNK])
        z = sb("z", [P, TILES, H])
        h2 = z
        h2_hi = sb("h2_hi", [P, TILES, H], F32R)
        h2_lo = sb("h2_lo", [P, TILES, H], F32R)
        xn = sb("xn", [P, TILES, H])
        h2T = xn[:, :, :].rearrange("p t (k n) -> p t k n", k=HK)
        xnT = sb("xnT", [P, HK, N])
        uT = sb("uT", [P, EK, N])
        v = sb("v", [P, TILES, E_DIM])
        hid = v[:, :, :].rearrange("p t e -> p (t e)").rearrange("p (b k c) -> p b k c", b=2, k=DK)
        rotary = sb("rotary", [P, 6, N])
        base = rotary[:, 0:2, :]
        qk = rotary[:, 2:4, :]
        qk_sw = rotary[:, 4:6, :]
        b2 = rotary[:, 0:4, :].rearrange("p a n -> p (a n)").rearrange("p (e h) -> p e h", e=EXP)
        yc = rotary[:, 4, :].rearrange("p (b h) -> p b h", b=2)
        result = rotary[:, 5, :].rearrange("p (b h) -> p b h", b=2)
        att = sb("att", [P, TILES, P])
        onehot = sb("onehot", [P, TILES + 2, HALF], F32R)
        xc = sb("xc", [P, 2, HK, CHUNK])
        rows_c = sb("rows_c", [3, 2, CHUNK])
        wt = sb("wt", [P, 2, 2])
        token_u = sb("token_u", [P, 2], U32)
        b1_more = sb("b1_more", [P, MORE, DK])
        b2_more = uT[:, 0:2, :].rearrange("p a n -> p (a n)")[:, 0:MORE * H].rearrange("p (m h) -> p m h", m=MORE)
        LNS = 2 * TILES + EXP + MORE
        stats = sb("stats", [P, LNS, 6])
        mv = sb("mv", [P, LNS, 2])
        vare = sb("vare", [P, LNS])
        rstd = sb("rstd", [P, LNS])
        logit = sb("logit", [P, TILES, EXP])
        top = sb("top", [P, TILES])
        ntop = sb("ntop", [P, TILES])
        expl = sb("expl", [P, TILES, EXP])
        expsum = sb("expsum", [P, TILES])
        weight = sb("weight", [P, TILES])
        cand = sb("cand", [P, TILES, EXP])
        first = sb("first", [P, TILES])
        chosen = sb("chosen", [P, TILES, EXP], BF16)
        before = sb("before", [P, TILES, EXP], BF16)
        mine = sb("mine", [P, TILES, EXP])
        slot = sb("slot", [P, TILES])
        parts = sb("parts", [P, TILES, P], F32R)
        offs = sb("offs", [1, EXP])
        zero32 = sb("zero32", [1, EXP * MAXC])
        total = sb("total", [1, EXP])
        over = sb("over", [1, EXP, MAXC])
        place = sb("place", [1, EXP * MAXC])
        from_a = sb("from_a", [1, EXP, MAXC])
        end = sb("end", [1, EXP])
        pick = sb("pick", [1, 1, MORE, EXP * MAXC])
        pick2 = sb("pick2", [1, 2, MORE, EXP * MAXC])
        meta_f = sb("meta_f", [1, 16])
        meta = sb("meta", [1, 16], I32)
        M_MORE, M_EXPERT, M_FROM = EXP, EXP + 1, EXP + 1 + MORE

        in_x = [sem(f"in_x{k}") for k in range(FK)]
        in_const = sem("in_const")
        in_cols = sem("in_cols")
        in_bias = sem("in_bias")
        in_rows = sem("in_rows")
        in_uv = sem("in_uv")
        in_u = sem("in_u")
        in_embed_rows = sem("in_embed_rows")
        in_ow = sem("in_ow")
        in_gate = sem("in_gate")
        in_b2 = sem("in_b2")
        in_w = [sem(f"in_w{e}") for e in range(EXP)]
        made_const = sem("made_const")
        warmed = sem("warmed")
        emb_done = sem("emb_done")
        z0_ready = sem("z0_ready")
        stats_done = sem("stats_done")
        mv_ready = sem("mv_ready")
        vare_ready = sem("vare_ready")
        rstd_ready = sem("rstd_ready")
        xn_ready = sem("xn_ready")
        xnT_done = sem("xnT_done")
        xnT_ready = sem("xnT_ready")
        v_done = sem("v_done")
        vpre_ready = sem("vpre_ready")
        v_ready = sem("v_ready")
        base_done = sem("base_done")
        base_ready = sem("base_ready")
        affine_ready = sem("affine_ready")
        rope_a = sem("rope_a")
        rope_b = sem("rope_b")
        qk_ready = sem("qk_ready")
        u_done = sem("u_done")
        u_ready = sem("u_ready")
        score_done = sem("score_done")
        biased = sem("biased")
        clipped = sem("clipped")
        att_ready = sem("att_ready")
        av_done = sem("av_done")
        gated = sem("gated")
        o_done = sem("o_done")
        z_ready = sem("z_ready")
        h2_ready = sem("h2_ready")
        h2T_done = sem("h2T_done")
        h2T_ready = sem("h2T_ready")
        logit_done = sem("logit_done")
        route = sem("route")
        ntop_ready = sem("ntop_ready")
        split_hi = sem("split_hi")
        split_lo = sem("split_lo")
        weight_hi = sem("weight_hi")
        parts_ready = sem("parts_ready")
        zeroed = sem("zeroed")
        rows_ready = sem("rows_ready")
        onehot_used = sem("onehot_used")
        exp_ready = sem("exp_ready")
        chosen_ready = sem("chosen_ready")
        rank_done = sem("rank_done")
        onehot_ready = sem("onehot_ready")
        meta_ready = sem("meta_ready")
        sort_done = sem("sort_done")
        xs_ready = sem("xs_ready")
        xc_ready = sem("xc_ready")
        rows_c_ready = sem("rows_c_ready")
        hid_done = sem("hid_done")
        hid_ready_a = sem("hid_ready_a")
        hid_ready_d = sem("hid_ready_d")
        b_more = sem("b_more")
        yc_done = sem("yc_done")
        turned = sem("turned")
        wt_ready = sem("wt_ready")
        token_ready = sem("token_ready")
        rest_ready = sem("rest_ready")
        mixed = sem("mixed")
        result_ready = sem("result_ready")
        out_stored = sem("out_stored")

        block = ctx.enter_context(nc.Block())

        def tile(t):
            return slice(t * P, (t + 1) * P)

        def emb_bank(t):
            return bank[(0, 1, 6, 7)[t]][:, 0:H]

        def xnT_bank(t):
            return bank[2 + t % 2][:, 0:H].rearrange("p (k n) -> p k n", k=HK)

        def v_bank(t):
            return bank[4 + t % 2][:, :]

        base_bank = bank[6]

        def u_bank(m):
            return bank[(7, 0, 1, 2)[m]][:, :]

        def score_bank(t):
            return bank[(3, 3, 6, 6)[t]][:, (t % 2) * P:(t % 2 + 1) * P]

        def av_bank(t):
            return bank[(4, 5, 3, 6)[t]][:, :]

        def o_bank(t):
            return bank[(0, 1, 7, 2)[t]][:, 0:H]

        def h2T_bank(t):
            return bank[(3, 6, 0, 1)[t]][:, 0:H].rearrange("p (k n) -> p k n", k=HK)

        logit_bank = bank[4][:, 0:TILES * EXP]
        place_bank = bank[5][:, 0:(TILES + 2) * EXP]

        def sort_bank(half, m):
            return bank[((6, 7), (2, 3))[half][m]][:, 0:HALF]

        def onehot_of(half, t):
            return onehot[:, (half * TILES + t) % (TILES + 2), :]

        rows_bank = bank[4]

        def hid_bank(n, half):
            return bank[(0, 1, 2, 3)[2 * (n % 2) + half]]

        def yc_bank(n):
            return bank[4 + n % 2][:, 0:H]

        def token_bank(n):
            return bank[6 + n % 2][:, 0:H + 2]

        @block.sync
        def _(sp):
            for k in range(FK):
                sp.dma_start(x_in[:, k, :], xT[:, k, :]).then_inc(in_x[k], 16)
            sp.wait_ge(in_x[FK - 3], 32)
            sp.dma_start(w_uv[:, :, E_DIM:], uvT[:, :, E_DIM:]).then_inc(in_uv, 16)
            sp.dma_start(w_uv[:, :, 0:E_DIM], uvT[:, :, 0:E_DIM]).then_inc(in_u, 16)
            sp.dma_start(w_o, owT).then_inc(in_ow, 16)
            sp.wait_ge(in_gate, 16)
            sp.wait_ge(in_bias, 16)
            for e in range(6):
                sp.dma_start(slots[:, e, :], expw[e]).then_inc(in_w[e], 16)
            sp.wait_ge(u_done, EK)
            sp.dma_start(slots[:, 6, :], expw[6]).then_inc(in_w[6], 16)
            sp.wait_ge(score_done, TILES)
            sp.dma_start(rotary[:, 0:4, :].rearrange("p a n -> p (a n)"), b2_d.partition_broadcast(P)).then_inc(in_b2, 16)
            sp.wait_ge(o_done, TILES)
            sp.dma_start(slots[:, 7, :], expw[7]).then_inc(in_w[7], 16)

            sp.wait_ge(meta_ready, 1)
            more = sp.value_load(meta[0:1, M_MORE:M_MORE + 1], min_val=0, max_val=MORE)
            for m in range(MORE):
                with sp.If(more > m):
                    e = sp.value_load(meta[0:1, M_EXPERT + m:M_EXPERT + m + 1], min_val=0, max_val=EXP - 1)
                    sp.wait_ge(yc_done, m + 1)
                    sp.dma_start(slots[:, m, :], expw[bass.ds(e, 1)].rearrange("a p n -> (a p) n"))\
                        .then_inc(in_w[m], 16)

        @block.gpsimd
        def _(pool):
            pool.memset(ones[:, :], 1.0).then_inc(made_const, 1)
            pool.memset(minus_half[:, :], -0.5).then_inc(made_const, 1)
            pool.memset(zero32[:, :], 0.0).then_inc(made_const, 1)
            pool.memset(parts[:, :, :].bitcast(F32), 0.0).then_inc(made_const, 1)
            pool.wait_ge(made_const, 4)
            pool.affine_select(out=upper[:, :], in_=ones[:, :], compare_op=ALU.is_gt, fill=0.0, base=0,
                               pattern=[[1, P]], channel_multiplier=-1).then_inc(made_const, 1)
            pool.iota(iota[:, :], [[1, N]], base=0, channel_multiplier=0,
                      allow_small_or_imprecise_dtypes=True).then_inc(made_const, 1)

            def rsqrt(i):
                pool.wait_ge(mv_ready, i + 1)
                pool.tensor_scalar(vare[:, i:i + 1], mv[:, i, 1:2], EPS, None, ALU.add).then_inc(vare_ready, 1)
                pool.wait_ge(vare_ready, i + 1)
                pool.tensor_tensor(rstd[:, i:i + 1], vare[:, i:i + 1], minus_half[:, :], ALU.pow)\
                    .then_inc(rstd_ready, 1)

            for t in range(TILES):
                rsqrt(t)
            pool.memset(xs[:, :, N:], 0.0).then_inc(zeroed, 1)
            pool.wait_ge(z0_ready, TILES)
            pool.wait_ge(vpre_ready, TILES)
            pool.memset(slot_rows[:, N:], float(2 * N)).then_inc(zeroed, 1)
            for t in range(TILES):
                rsqrt(TILES + t)

            def store(n):
                rsqrt(2 * TILES + n)
                pool.wait_ge(result_ready, n + 1)
                pool.wait_ge(token_ready, n + 1)
                if n:
                    pool.wait_ge(out_stored, 16 * n)
                pool.indirect_dma_start(out, bass.IndirectOffsetOnAxis(ap=token_u[:, n % 2:n % 2 + 1], axis=0),
                                        result[:, n % 2, :], None, bounds_check=N - 1, oob_is_err=False)\
                    .then_inc(out_stored, 16)

            for n in range(EXP):
                store(n)
            pool.wait_ge(meta_ready, 1)
            more = pool.value_load(meta[0:1, M_MORE:M_MORE + 1], min_val=0, max_val=MORE)
            for m in range(MORE):
                with pool.If(more > m):
                    store(EXP + m)
            pool.wait_ge(out_stored, 16 * EXP)
            for m in range(MORE):
                with pool.If(more > m):
                    pool.wait_ge(out_stored, 16 * (EXP + m + 1))

        @block.scalar
        def _(act):
            act.dma_start(embed_rows[:, :], embed_rows_d).then_inc(in_embed_rows, 16)
            for k in range(FK):
                act.dma_start(w_emb[:, k, :], wT[:, k, :]).then_inc(in_x[k], 16)
            act.dma_start(const[:, :], const_d).then_inc(in_const, 16)
            act.dma_start(cols[:, :], cols_d).then_inc(in_cols, 16)
            act.dma_start(rows[:, :], rows_d.partition_broadcast(P)).then_inc(in_rows, 16)
            act.dma_start(rel_bias[:, :], biasT_d).then_inc(in_bias, 16)
            act.dma_start(gate[:, :, :], gateT).then_inc(in_gate, 16)

            act.wait_ge(made_const, 2)
            act.activation(warm[:, :], minus_half[:, :], ACT.Silu).then_inc(warmed, 1)
            act.wait_ge(in_cols, 16)
            def xnT_copy(t):
                act.wait_ge(xnT_done, t + 1)
                for m in range(HK):
                    act.activation(xnT[:, m, tile(t)], xnT_bank(t)[:, m, :], ACT.Identity,
                                   scale=col("ln_w", m), bias=col("ln_b", m)).then_inc(xnT_ready, 1)

            def v_silu(t):
                act.wait_ge(vpre_ready, t + 1)
                act.activation(v[:, t, :], v[:, t, :], ACT.Silu).then_inc(v_ready, 1)

            for t in range(TILES):
                xnT_copy(t)
            act.wait_ge(base_done, 1)
            act.activation(base[:, 0, :], base_bank[:, :], ACT.Silu, bias=col("base_b")).then_inc(base_ready, 1)
            for a, b in ((0, S // 2), (S // 2, 0)):
                act.activation(base[b:b + S // 2, 1, :], base_bank[a:a + S // 2, :], ACT.Silu,
                               bias=cols[a:a + S // 2, COLS["base_b"][0]:COLS["base_b"][0] + 1]).then_inc(base_ready, 1)
            act.wait_ge(base_ready, 3)
            for j in range(2):
                act.activation(qk[:, j, :], base[:, 0, :], ACT.Identity, scale=col("gamma", j), bias=col("beta", j))\
                    .then_inc(affine_ready, 1)
                act.activation(qk_sw[:, j, :], base[:, 1, :], ACT.Identity, scale=col("gamma_sw", j),
                               bias=col("beta_sw", j)).then_inc(affine_ready, 1)
            for t in range(TILES):
                v_silu(t)
            for m in range(EK):
                act.wait_ge(u_done, m + 1)
                act.activation(uT[:, m, :], u_bank(m), ACT.Silu, bias=col("u_b", m)).then_inc(u_ready, 1)
            for t in range(TILES):
                act.wait_ge(h2T_done, t + 1)
                act.activation(h2T[:, t, :, :], h2T_bank(t), ACT.Copy).then_inc(h2T_ready, 1)
                act.activation(h2_hi[:, t, :], h2[:, t, :], ACT.Copy).then_inc(split_hi, 1)
            for t in range(TILES):
                act.wait_ge(ntop_ready, 1)
                act.activation(expl[:, t, :], logit[:, t, :], ACT.Exp, bias=ntop[:, t:t + 1],
                               accum_out=expsum[:, t:t + 1]).then_inc(exp_ready, 1)
            act.wait_ge(sort_done, 1)
            act.activation(xc[:, 0, 0, :], sort_bank(0, 0)[:, 0:CHUNK], ACT.Copy).then_inc(xc_ready, 1)
            act.activation(xs[:, 0, 0:HALF], sort_bank(0, 0), ACT.Copy).then_inc(xs_ready, 1)
            act.wait_ge(sort_done, HK + 1)
            act.activation(xs[:, 0, HALF:N], sort_bank(1, 0), ACT.Copy).then_inc(xs_ready, 1)

            def hidden(n, b1_col):
                act.wait_ge(hid_done, 2 * n + 1)
                if n >= 2:
                    act.wait_ge(yc_done, n - 1)
                for c in range(DK // 2):
                    act.activation(hid[:, n % 2, c, :], hid_bank(n, 0)[:, c * CHUNK:(c + 1) * CHUNK], ACT.Relu,
                                   bias=b1_col(c)).then_inc(hid_ready_a, 1)

            for n in range(EXP):
                hidden(n, lambda c, n=n: col("b1", n * DK + c))
            act.wait_ge(meta_ready, 1)
            more = act.value_load(meta[0:1, M_MORE:M_MORE + 1], min_val=0, max_val=MORE)
            for m in range(MORE):
                with act.If(more > m):
                    act.wait_ge(b_more, 2 * m + 2)
                    hidden(EXP + m, lambda c, m=m: b1_more[:, m, c:c + 1])

        @block.tensor
        def _(pe):
            def embed(t, k):
                mm = pe.matmul(emb_bank(t), x_in[:, k, tile(t)], w_emb[:, k, :], start=False, stop=(k == FK - 1))
                if k == FK - 1:
                    mm.then_inc(emb_done, 1)

            pe.wait_ge(made_const, 1)
            for _ in range(WARMUP):
                pe.matmul(bank[5][:, :], ones[:, :], ones[:, :].unsqueeze(1).to_broadcast([P, 4, P]), start=True,
                          stop=True)
            pe.wait_ge(in_embed_rows, 16)
            for t in range(TILES):
                pe.matmul(emb_bank(t), token_pos, pos_and_b, start=True, stop=False)
            for k in range(FK // 2):
                pe.wait_ge(in_x[k], 32)
                for t in range(TILES):
                    embed(t, k)
            for t in range(TILES):
                for k in range(FK // 2, FK):
                    if t == 0:
                        pe.wait_ge(in_x[k], 32)
                    embed(t, k)
            pe.wait_ge(in_const, 16)

            def turn_xn(t):
                pe.wait_ge(xn_ready, t + 1)
                if t >= 2:
                    pe.wait_ge(xnT_ready, HK * (t - 1))
                for m in range(HK):
                    tr = pe.transpose(xnT_bank(t)[:, m, :], xn[:, t, tile(m)], ident)
                tr.then_inc(xnT_done, 1)

            def v_product(t):
                pe.wait_ge(xnT_ready, HK * (t + 1))
                if t >= 2:
                    pe.wait_ge(vpre_ready, t - 1)
                for k in range(HK):
                    mm = pe.matmul(v_bank(t), xnT[:, k, tile(t)], w_uv[:, k, E_DIM:2 * E_DIM], start=(k == 0),
                                   stop=(k == HK - 1))
                mm.then_inc(v_done, 1)

            def u_product(m):
                for k in range(HK):
                    mm = pe.matmul(u_bank(m), w_uv[:, k, m * P:(m + 1) * P], xnT[:, k, :], start=(k == 0),
                                   stop=(k == HK - 1))
                mm.then_inc(u_done, 1)

            turn_xn(0)
            turn_xn(1)
            pe.wait_ge(in_uv, 16)
            v_product(0)
            turn_xn(2)
            turn_xn(3)
            v_product(1)
            pe.wait_ge(xnT_ready, HK * TILES)
            pe.wait_ge(z0_ready, TILES)
            for k in range(HK):
                mm = pe.matmul(base_bank[:, :], w_uv[:, k, 2 * E_DIM:UV], xnT[:, k, :], start=(k == 0),
                               stop=(k == HK - 1))
            mm.then_inc(base_done, 1)
            v_product(2)
            v_product(3)
            pe.wait_ge(in_u, 16)
            u_product(0)
            u_product(1)
            pe.wait_ge(qk_ready, 2)
            for t in range(TILES):
                pe.matmul(score_bank(t), qk[:, 1, tile(t)], qk[:, 0, tile(t)], start=True, stop=True)\
                    .then_inc(score_done, 1)
            u_product(2)
            u_product(3)

            def attend(t):
                pe.wait_ge(att_ready, t + 1)
                pe.wait_ge(v_ready, TILES)
                if t >= 2:
                    pe.wait_ge(att_ready, TILES)
                for m in range(EK):
                    mm = pe.matmul(av_bank(t)[:, tile(m)], v[:, t, tile(m)], att[:, t, :], start=True, stop=True)
                mm.then_inc(av_done, 1)

            def project(t):
                pe.wait_ge(gated, t + 1)
                pe.wait_ge(in_ow, 16)
                for m in range(EK):
                    mm = pe.matmul(o_bank(t), uT[:, m, tile(t)], w_o[:, m, :], start=(m == 0), stop=(m == EK - 1))
                mm.then_inc(o_done, 1)

            def turn_h2(t):
                pe.wait_ge(h2_ready, t + 1)
                for m in range(HK):
                    tr = pe.transpose(h2T_bank(t)[:, m, :], h2[:, t, tile(m)], ident)
                tr.then_inc(h2T_done, 1)

            def logits(t):
                pe.wait_ge(h2T_ready, t + 1)
                pe.wait_ge(in_gate, 16)
                for m in range(HK):
                    mm = pe.matmul(logit_bank[:, t * EXP:(t + 1) * EXP], h2T[:, t, m, :], gate[:, m, :],
                                   start=(m == 0), stop=(m == HK - 1))
                mm.then_inc(logit_done, 1)

            for t in range(TILES):
                attend(t)
            project(0)
            project(1)
            project(2)
            turn_h2(0)
            project(3)
            turn_h2(1)
            logits(0)
            turn_h2(2)
            logits(1)
            turn_h2(3)
            logits(2)
            logits(3)

            pe.wait_ge(made_const, 6)
            pe.wait_ge(chosen_ready, 2)
            blocks = TILES + 2
            by_tile = place_bank.rearrange("p (b e) -> p b e", b=blocks)
            for t in range(TILES):
                pe.matmul(by_tile[:, 0:TILES + 1, :], ones[:, :],
                          before[:, t:t + 1, :].to_broadcast([P, TILES + 1, EXP]),
                          start=(t == 0), stop=False, skip_group_check=True)
                pe.matmul(by_tile[:, TILES + 1, :], ones[:, :], chosen[:, t, :], start=False, stop=False,
                          skip_group_check=True)
                if t + 1 < TILES:
                    pe.matmul(by_tile[:, t + 1:TILES, :], ones[:, :],
                              chosen[:, t:t + 1, :].to_broadcast([P, TILES - 1 - t, EXP]),
                              start=False, stop=False, skip_group_check=True)
                last = pe.matmul(by_tile[:, t, :], upper[:, :], chosen[:, t, :], start=False,
                                 stop=(t == TILES - 1), skip_group_check=True)
            last.then_inc(rank_done, 1)

            def sort(half, t):
                pe.wait_ge(onehot_ready, half * TILES + t + 1)
                pe.wait_ge(split_lo, t + 1)
                for m in range(HK):
                    for part in (h2_hi, h2_lo):
                        mm = pe.matmul(sort_bank(half, m), part[:, t, tile(m)], onehot_of(half, t),
                                       start=(t == 0 and part is h2_hi), stop=(t == TILES - 1 and part is h2_lo))
                    if t == TILES - 1:
                        mm.then_inc(sort_done, 1)

            def sort_rows(half, t):
                pe.wait_ge(parts_ready, 2)
                pe.matmul(rows_bank[:, half * HALF:(half + 1) * HALF], parts[:, t, :], onehot_of(half, t),
                          start=(t == 0), stop=(t == TILES - 1)).then_inc(onehot_used, 1)

            for t in range(TILES):
                sort(0, t)
            for t in range(TILES):
                sort_rows(0, t)
            for t in range(TILES):
                sort(1, t)
                sort_rows(1, t)

            def hidden(n, slot_):
                pe.wait_ge(xc_ready, n + 2)
                if n >= 2:
                    pe.wait_ge(hid_ready_a, DK // 2 * (n - 1))
                    pe.wait_ge(hid_ready_d, DK // 2 * (n - 1))
                for c in range(DK):
                    for k in range(HK):
                        mm = pe.matmul(hid_bank(n, c // 4)[:, (c % 4) * CHUNK:(c % 4 + 1) * CHUNK],
                                       w1(slot_)[:, k, c * P:(c + 1) * P], xc[:, n % 2, k, :], start=(k == 0),
                                       stop=(k == HK - 1))
                    if c % 4 == 3:
                        mm.then_inc(hid_done, 1)

            def turn(n):
                if n == 0:
                    pe.wait_ge(xs_ready, 4)
                if n >= 2:
                    pe.wait_ge(rest_ready, n - 1)
                for k in range(HK):
                    pe.transpose(token_bank(n)[:, tile(k)], xc[:, n % 2, k, :], ident)
                pe.wait_ge(rows_c_ready, n + 1)
                pe.matmul(token_bank(n)[:, H:H + 2], rows_c[:, n % 2, :], con("sum_parts", 3), start=True, stop=True)\
                    .then_inc(turned, 1)

            def output(n, slot_):
                if n == 0:
                    pe.wait_ge(rows_ready, 1)
                if n >= 2:
                    pe.wait_ge(mixed, n - 1)
                for c in range(DK):
                    if c % 4 == 0:
                        pe.wait_ge(hid_ready_d if c else hid_ready_a, DK // 2 * (n + 1))
                    mm = pe.matmul(yc_bank(n), hid[:, n % 2, c, :], w2(slot_)[:, c, :], start=(c == 0),
                                   stop=(c == DK - 1))
                mm.then_inc(yc_done, 1)

            for n in range(EXP):
                if n == EXP - 1:
                    pe.wait_ge(meta_ready, 1)
                    more = pe.value_load(meta[0:1, M_MORE:M_MORE + 1], min_val=0, max_val=MORE)
                pe.wait_ge(in_w[n], 16)
                hidden(n, n)
                turn(n)
                if n:
                    output(n - 1, n - 1)
            for m in range(MORE):
                with pe.If(more > m):
                    pe.wait_ge(in_w[m], 32)
                    hidden(EXP + m, m)
                    turn(EXP + m)
                if m == 0:
                    output(EXP - 1, EXP - 1)
                else:
                    with pe.If(more > m - 1):
                        output(EXP + m - 1, m - 1)
            with pe.If(more > MORE - 1):
                output(EXP + MORE - 1, MORE - 1)

        @block.vector
        def _(dve):
            def moments(i, src):
                dve.bn_stats(stats[:, i, :], src).then_inc(stats_done, 1)
                dve.wait_ge(stats_done, i + 1)
                dve.bn_aggr(mv[:, i, :], stats[:, i, :]).then_inc(mv_ready, 1)

            def normalise(i, dst, src, done):
                dve.wait_ge(mv_ready, i + 1)
                dve.wait_ge(rstd_ready, i + 1)
                dve.tensor_scalar(dst, src, mv[:, i, 0:1], rstd[:, i:i + 1], ALU.subtract, ALU.mult).then_inc(done, 1)

            for t in range(TILES + 1):
                if t < TILES:
                    dve.wait_ge(emb_done, t + 1)
                    moments(t, emb_bank(t))
                if t:
                    normalise(t - 1, xn[:, t - 1, :], emb_bank(t - 1), xn_ready)
            dve.wait_ge(in_rows, 16)
            for t in range(TILES):
                dve.scalar_tensor_tensor(out=z[:, t, :], in0=emb_bank(t), scalar=2.0, in1=o_b, op0=ALU.mult,
                                         op1=ALU.add).then_inc(z0_ready, 1)
            for t in range(TILES):
                dve.wait_ge(v_done, t + 1)
                dve.tensor_tensor(v[:, t, :], v_bank(t), v_b, ALU.add).then_inc(vpre_ready, 1)

            def over_images(name):
                return con(name).unsqueeze(1).to_broadcast([P, IMAGES, TOK])

            def by_image(ap):
                return ap.rearrange("p (i t) -> p i t", i=IMAGES)

            dve.wait_ge(in_const, 16)
            for j in range(2):
                dve.wait_ge(affine_ready, 2 * j + 1)
                dve.tensor_tensor(by_image(qk[:, j, :]), by_image(qk[:, j, :]), over_images("cos"), ALU.mult)\
                    .then_inc(rope_a, 1)
                dve.wait_ge(affine_ready, 2 * j + 2)
                dve.tensor_tensor(by_image(qk_sw[:, j, :]), by_image(qk_sw[:, j, :]), over_images("sin"), ALU.mult)\
                    .then_inc(rope_b, 1)
                dve.wait_ge(rope_a, j + 1)
                dve.wait_ge(rope_b, j + 1)
                dve.tensor_tensor(qk[:, j, :], qk[:, j, :], qk_sw[:, j, :], ALU.add).then_inc(qk_ready, 1)

            for t in range(TILES):
                dve.wait_ge(in_bias, 16)
                dve.wait_ge(score_done, 2 * (t // 2) + 2)
                dve.scalar_tensor_tensor(out=att[:, t, :], in0=score_bank(t), scalar=1.0 / float(np.sqrt(S)),
                                         in1=rel_bias[:, :], op0=ALU.mult, op1=ALU.add).then_inc(biased, 1)
                dve.wait_ge(biased, t + 1)
                dve.scalar_tensor_tensor(out=att[:, t, :], in0=att[:, t, :], scalar=0.0, in1=con("block"),
                                         op0=ALU.max, op1=ALU.mult).then_inc(clipped, 1)
                dve.wait_ge(clipped, t + 1)
                dve.tensor_tensor(att[:, t, :], att[:, t, :], att[:, t, :], ALU.mult).then_inc(att_ready, 1)

            def gate_u(t):
                dve.wait_ge(av_done, t + 1)
                dve.wait_ge(u_ready, EK)
                dve.tensor_tensor(uT[:, :, tile(t)], uT[:, :, tile(t)],
                                  av_bank(t).rearrange("p (m n) -> p m n", m=EK), ALU.mult).then_inc(gated, 1)

            def residual(t):
                dve.wait_ge(o_done, t + 1)
                dve.wait_ge(z0_ready, t + 1)
                dve.tensor_tensor(z[:, t, :], z[:, t, :], o_bank(t), ALU.add).then_inc(z_ready, 1)
                dve.wait_ge(z_ready, t + 1)
                moments(TILES + t, z[:, t, :])

            def norm2(t):
                normalise(TILES + t, h2[:, t, :], z[:, t, :], h2_ready)

            def rest_of_h2(t):
                dve.wait_ge(split_hi, t + 1)
                dve.tensor_tensor(h2_lo[:, t, :], h2[:, t, :], h2_hi[:, t, :].bitcast(F32), ALU.subtract)\
                    .then_inc(split_lo, 1)

            for t in range(TILES):
                gate_u(t)
            residual(0)
            residual(1)
            norm2(0)
            residual(2)
            norm2(1)
            rest_of_h2(0)
            residual(3)
            norm2(2)
            norm2(3)

            step = [0]

            def then(ins):
                step[0] += 1
                ins.then_inc(route, 1)
                dve.wait_ge(route, step[0])

            rest_of_h2(1)
            rest_of_h2(2)
            logits = logit_bank.rearrange("p (t e) -> p t e", t=TILES)
            rev = con("rev").unsqueeze(1).to_broadcast([P, TILES, EXP])

            def per_tile(ap):
                return ap.unsqueeze(2).to_broadcast([P, TILES, EXP])

            dve.wait_ge(logit_done, TILES)
            then(dve.tensor_reduce(top[:, :], logits, AX_X, ALU.max))
            then(dve.tensor_tensor(cand[:, :, :], logits, per_tile(top[:, :]), ALU.is_equal))
            then(dve.tensor_tensor(cand[:, :, :], cand[:, :, :], rev, ALU.mult))
            then(dve.tensor_reduce(first[:, :], cand[:, :, :], AX_X, ALU.max))
            dve.tensor_tensor(before[:, :, :], rev, per_tile(first[:, :]), ALU.is_lt).then_inc(chosen_ready, 1)
            dve.tensor_tensor(chosen[:, :, :], rev, per_tile(first[:, :]), ALU.is_equal).then_inc(chosen_ready, 1)
            then(dve.tensor_copy(logit[:, :, :], logits))
            dve.tensor_scalar(ntop[:, :], top[:, :], -1.0, None, ALU.mult).then_inc(ntop_ready, 1)
            dve.wait_ge(chosen_ready, 2)
            dve.wait_ge(rank_done, 1)
            places = place_bank.rearrange("p (b e) -> p b e", b=TILES + 2)
            then(dve.tensor_tensor(mine[:, :, :], places[:, 0:TILES, :], chosen[:, :, :], ALU.mult))
            then(dve.tensor_reduce(slot[:, :], mine[:, :, :], AX_X, ALU.add))

            dve.wait_ge(made_const, 6)

            def make_onehot(half, t):
                if half and t >= 2:
                    dve.wait_ge(onehot_used, t - 1)
                dve.tensor_scalar(onehot_of(half, t), iota[:, half * HALF:(half + 1) * HALF], slot[:, t:t + 1], None,
                                  ALU.is_equal).then_inc(onehot_ready, 1)

            for t in range(TILES):
                make_onehot(0, t)
            rest_of_h2(3)
            dve.wait_ge(exp_ready, TILES)
            then(dve.reciprocal(weight[:, :], expsum[:, :]))
            dve.tensor_copy(parts[:, :, 0], weight[:, :]).then_inc(weight_hi, 1)
            dve.tensor_copy(parts[:, :, 2], con("token")).then_inc(parts_ready, 1)
            dve.wait_ge(weight_hi, 1)
            dve.tensor_tensor(parts[:, :, 1], weight[:, :], parts[:, :, 0].bitcast(F32), ALU.subtract)\
                .then_inc(parts_ready, 1)
            then(dve.tensor_copy(offs[:, :], places[0:1, TILES, :]))
            then(dve.tensor_copy(total[:, :], places[0:1, TILES + 1, :]))
            then(dve.tensor_copy(meta[:, 0:EXP], offs[:, :]))
            for t in range(TILES):
                make_onehot(1, t)
            dve.wait_ge(sort_done, 2)
            dve.tensor_copy(xc[:, 0, 1, :], sort_bank(0, 1)[:, 0:CHUNK]).then_inc(xc_ready, 1)
            dve.tensor_copy(xs[:, 1, 0:HALF], sort_bank(0, 1)).then_inc(xs_ready, 1)

            dve.wait_ge(sort_done, 2 * HK)
            dve.tensor_copy(xs[:, 1, HALF:N], sort_bank(1, 1)).then_inc(xs_ready, 1)
            dve.wait_ge(zeroed, 2)
            dve.wait_ge(onehot_used, 2 * TILES)
            dve.tensor_copy(slot_rows[:, 0:N], rows_bank[0:3, :]).then_inc(rows_ready, 1)
            dve.wait_ge(rows_ready, 1)
            dve.wait_ge(xs_ready, 4)

            def fetch_chunk(n, at):
                start = dve.value_load(meta[0:1, at:at + 1], min_val=0, max_val=N)
                if n >= 2:
                    dve.wait_ge(hid_done, 2 * (n - 1))
                    dve.wait_ge(turned, n - 1)
                if n:
                    dve.tensor_copy(xc[:, n % 2, :, :], xs[:, :, bass.ds(start, CHUNK)]).then_inc(xc_ready, 1)
                dve.tensor_copy(rows_c[:, n % 2, :], slot_rows[:, bass.ds(start, CHUNK)]).then_inc(rows_c_ready, 1)

            def fetch_more(m):
                fetch_chunk(EXP + m, M_FROM + m)
                e = dve.value_load(meta[0:1, M_EXPERT + m:M_EXPERT + m + 1], min_val=0, max_val=EXP - 1)
                b1_all = col("b1", 0, EXP * DK).rearrange("p (e c) -> p e c", e=EXP)
                dve.tensor_copy(b1_more[:, m:m + 1, :], b1_all[:, bass.ds(e, 1), :]).then_inc(b_more, 1)
                dve.tensor_copy(b2_more[:, m:m + 1, :], b2[:, bass.ds(e, 1), :]).then_inc(b_more, 1)

            def hidden(n, b1_col):
                dve.wait_ge(hid_done, 2 * n + 2)
                if n >= EXP:
                    dve.wait_ge(b_more, 2 * (n - EXP) + 2)
                if n >= 2:
                    dve.wait_ge(yc_done, n - 1)
                for c in range(DK // 2, DK):
                    dve.tensor_scalar(hid[:, n % 2, c, :], hid_bank(n, 1)[:, (c - 4) * CHUNK:(c - 3) * CHUNK],
                                      b1_col(c), 0.0, ALU.add, ALU.max).then_inc(hid_ready_d, 1)

            def rest(n, b2_row):
                dve.wait_ge(turned, n + 1)
                if n >= 2:
                    dve.wait_ge(out_stored, 16 * (n - 1))
                dve.tensor_copy(wt[:, n % 2, :], token_bank(n)[:, H:H + 2]).then_inc(wt_ready, 1)
                dve.tensor_copy(token_u[:, n % 2:n % 2 + 1], token_bank(n)[:, H + 1:H + 2]).then_inc(token_ready, 1)
                dve.wait_ge(wt_ready, n + 1)
                dve.scalar_tensor_tensor(out=yc[:, n % 2, :], in0=b2_row, scalar=wt[:, n % 2, 0:1],
                                         in1=token_bank(n)[:, 0:H], op0=ALU.mult, op1=ALU.add).then_inc(rest_ready, 1)

            def output(n):
                dve.wait_ge(yc_done, n + 1)
                dve.wait_ge(rest_ready, n + 1)
                dve.scalar_tensor_tensor(out=yc[:, n % 2, :], in0=yc_bank(n), scalar=wt[:, n % 2, 0:1],
                                         in1=yc[:, n % 2, :], op0=ALU.mult, op1=ALU.add).then_inc(mixed, 1)
                dve.wait_ge(mixed, n + 1)
                moments(2 * TILES + n, yc[:, n % 2, :])
                normalise(2 * TILES + n, result[:, n % 2, :], yc[:, n % 2, :], result_ready)

            def count_more():
                by_expert = [1, EXP, MAXC]

                def spread(ap):
                    return ap.unsqueeze(2).to_broadcast(by_expert)

                thr = con("thr", 1).rearrange("p (e c) -> p e c", e=EXP)
                then(dve.tensor_tensor(end[:, :], offs[:, :], total[:, :], ALU.add))
                then(dve.tensor_tensor(over[:, :, :], spread(total[:, :]), thr, ALU.is_gt))
                over_row = over[:, :, :].rearrange("p e c -> p (e c)")
                then(dve.tensor_tensor_scan(place[:, :], over_row, zero32[:, :], 0.0, ALU.add, ALU.add))
                then(dve.tensor_copy(meta_f[:, M_MORE:M_MORE + 1], place[:, EXP * MAXC - 1:EXP * MAXC]))
                then(dve.tensor_tensor(place[:, :], place[:, :], over_row, ALU.mult))
                then(dve.tensor_tensor(from_a[:, :, :], spread(offs[:, :]), thr, ALU.add))
                then(dve.tensor_scalar(end[:, :], end[:, :], float(-CHUNK), None, ALU.add))
                then(dve.tensor_tensor(from_a[:, :, :], from_a[:, :, :], spread(end[:, :]), ALU.min))
                nth = con("nth", 1).rearrange("p (m i) -> p m i", m=MORE)

                def for_each(ap):
                    return ap.unsqueeze(1).to_broadcast([1, MORE, EXP * MAXC])

                then(dve.tensor_tensor(pick[:, 0, :, :], for_each(place[:, :]), nth, ALU.is_equal))
                then(dve.tensor_tensor(pick2[:, 0, :, :], pick[:, 0, :, :], for_each(con("expert", 1)), ALU.mult))
                then(dve.tensor_tensor(pick2[:, 1, :, :], pick[:, 0, :, :],
                                       for_each(from_a[:, :, :].rearrange("p e c -> p (e c)")), ALU.mult))
                then(dve.tensor_reduce(meta_f[:, M_EXPERT:M_EXPERT + 2 * MORE],
                                       pick2[:, :, :, :].rearrange("p a m i -> p (a m) i"), AX_X, ALU.add))
                dve.tensor_copy(meta[:, M_MORE:M_MORE + 1 + 2 * MORE], meta_f[:, M_MORE:M_MORE + 1 + 2 * MORE])\
                    .then_inc(meta_ready, 1)
                dve.wait_ge(meta_ready, 1)

            dve.wait_ge(in_b2, 16)
            dve.wait_ge(in_cols, 16)
            fetch_chunk(0, 0)
            fetch_chunk(1, 1)
            for n in range(EXP):
                if n:
                    rest(n - 1, b2[:, n - 1, :])
                hidden(n, lambda c, n=n: col("b1", n * DK + c))
                if n == 0:
                    count_more()
                if n == EXP - 2:
                    more = dve.value_load(meta[0:1, M_MORE:M_MORE + 1], min_val=0, max_val=MORE)
                if n + 2 < EXP:
                    fetch_chunk(n + 2, n + 2)
                else:
                    with dve.If(more > n + 2 - EXP):
                        fetch_more(n + 2 - EXP)
                if n:
                    output(n - 1)
            rest(EXP - 1, b2[:, EXP - 1, :])
            for m in range(MORE):
                with dve.If(more > m):
                    hidden(EXP + m, lambda c, m=m: b1_more[:, m, c:c + 1])
                if m + 2 < MORE:
                    with dve.If(more > m + 2):
                        fetch_more(m + 2)
                if m == 0:
                    output(EXP - 1)
                else:
                    with dve.If(more > m - 1):
                        output(EXP + m - 1)
                with dve.If(more > m):
                    rest(EXP + m, b2_more[:, m, :])
            with dve.If(more > MORE - 1):
                output(EXP + MORE - 1)


def kernel(x, L0_tok_W, L0_tok_b, L0_tok_pos_emb, L0_attn_ln_w, L0_attn_ln_b, L0_attn_uv_w, L0_attn_uv_b,
           L0_attn_gamma, L0_attn_beta, L0_attn_w, L0_attn_o_w, L0_attn_o_b, L0_ffn_gate_w, L0_ffn_w1, L0_ffn_b1,
           L0_ffn_w2, L0_ffn_b2):
    import concourse.bacc as bacc
    from concourse.bass_utils import run_bass_kernel_spmd

    def chunks(a):
        a = np.asarray(a)
        return np.ascontiguousarray(a.reshape(a.shape[0] // P, P, a.shape[1]).transpose(1, 0, 2))

    def column(a):
        return np.asarray(a).reshape(-1, P).T

    def swap(a):
        return np.concatenate([a[S // 2:], a[:S // 2]])

    patches = np.asarray(x).reshape(IMAGES, CH, SIDE, PATCH, SIDE, PATCH).transpose(0, 2, 4, 1, 3, 5).reshape(N, FEAT)
    uv_b = np.asarray(L0_attn_uv_b)
    gamma, beta = np.asarray(L0_attn_gamma).T, np.asarray(L0_attn_beta).T
    base_b = uv_b[2 * E_DIM:].reshape(S, 1)
    cols = {"ln_w": column(L0_attn_ln_w), "ln_b": column(L0_attn_ln_b), "u_b": column(uv_b[:E_DIM]),
            "base_b": base_b, "base_b_sw": swap(base_b), "gamma": gamma, "beta": beta, "gamma_sw": swap(gamma),
            "beta_sw": swap(beta), "b1": column(np.asarray(L0_ffn_b1).reshape(-1))}
    local = np.arange(P) % TOK
    w1 = np.asarray(L0_ffn_w1).reshape(EXP, HK, P, DFF).transpose(0, 2, 1, 3).reshape(EXP, P, HK * DFF)
    w2 = np.asarray(L0_ffn_w2).reshape(EXP, DK, P, H).transpose(0, 2, 1, 3).reshape(EXP, P, DK * H)
    arrays = {
        "patchesT": chunks(patches.T),
        "embed_wT": chunks(np.asarray(L0_tok_W).T),
        "uv_wT": chunks(np.asarray(L0_attn_uv_w).T),
        "o_wT": chunks(np.asarray(L0_attn_o_w).T),
        "gate_wT": chunks(np.asarray(L0_ffn_gate_w).T),
        "expert_w": np.concatenate([w1, w2], axis=2),
        "param_cols": np.concatenate([cols[name] for name in COLS], axis=1),
        "param_rows": np.concatenate([np.asarray(L0_attn_o_b), uv_b[E_DIM:2 * E_DIM]]),
        "embed_rows": np.concatenate([
            np.concatenate([np.asarray(L0_tok_pos_emb).reshape(TOK, H), np.asarray(L0_tok_b)[None, :]]),
            np.concatenate([local[None, :] == np.arange(TOK)[:, None], np.ones((1, P), bool)]).astype(np.float32)],
            axis=1),
        "rel_bias": np.asarray(L0_attn_w)[local[:, None] - local[None, :] + BIAS_LEN - 1],
        "expert_b2": np.asarray(L0_ffn_b2).reshape(-1),
        "consts": constant_table(),
    }
    nc = bacc.Bacc("TRN2", target_bir_lowering=False, num_devices=1)
    arrays = {k: np.ascontiguousarray(a) for k, a in arrays.items()}
    ins = [nc.dram_tensor(f"{k}_d", a.shape, mybir.dt.from_np(a.dtype), kind="ExternalInput").ap() for k, a in arrays.items()]
    out = nc.dram_tensor("out", [N, H], F32, kind="ExternalOutput").ap()
    build(nc, *ins, out)
    r = run_bass_kernel_spmd(nc, [{f"{k}_d": a for k, a in arrays.items()}], core_ids=[0])
    return r.results[0]["out"].reshape(IMAGES, TOK, H)
```

```python
from contextlib import ExitStack

import numpy as np

import concourse.bass as bass
from concourse import mybir

ALU = mybir.AluOpType
ACT = mybir.ActivationFunctionType
F32 = mybir.dt.float32
F32R = mybir.dt.float32r
BF16 = mybir.dt.bfloat16
I32 = mybir.dt.int32
U32 = mybir.dt.uint32
AX_X = mybir.AxisListType.X

P = 128
IMAGES, TOK, PATCH, CH, SIDE = 32, 16, 16, 3, 4
N = IMAGES * TOK
TILES = N // P
FEAT = CH * PATCH * PATCH
FK = FEAT // P
H = 256
HK = H // P
E_DIM = 512
EK = E_DIM // P
S = 128
UV = 2 * E_DIM + S
EXP = 8
HALF = N // 2
DFF = 1024
DK = DFF // P
BIAS_LEN = 128
EPS = 1e-5
CHUNK = 128
SLOTS = 6
MORE = sum(1 for c in range(1, N) if c * CHUNK + 1 <= N)
MAXC = N // CHUNK - 1
PHASE_K = 2
WARMUP = 7
WCOLS = HK * DFF + DK * H
DVE_K = 6

COLS = {}
_at = 0
for _name, _n in (("ln_w", HK), ("ln_b", HK), ("u_b", EK), ("base_b", 1), ("base_b_sw", 1), ("gamma", 2), ("beta", 2),
                  ("gamma_sw", 2), ("beta_sw", 2), ("b1", EXP * DK)):
    COLS[_name] = (_at, _n)
    _at += _n
NCOLS = _at
CONSTS = {}
_at = 0
for _name, _n in (("ident", P), ("block", P), ("cos", TOK), ("sin", TOK), ("rev", EXP), ("token", TILES),
                  ("sum_parts", 2), ("thr", EXP * MAXC), ("expert", EXP * MAXC), ("nth", MORE * EXP * MAXC)):
    CONSTS[_name] = (_at, _n)
    _at += _n
NCONSTS = _at


def constant_table():
    t = np.zeros((P, NCONSTS), np.float32)

    def put(name, value):
        a, n = CONSTS[name]
        t[:, a:a + n] = value

    put("ident", np.eye(P))
    i = np.arange(P)
    put("block", i[:, None] // TOK == i[None, :] // TOK)
    half = S // 2
    inv = (10000.0 ** (np.arange(half) / half)).astype(np.float32)
    angle = (np.arange(TOK, dtype=np.float32)[None, :] * inv[:, None]).astype(np.float32)
    put("cos", np.concatenate([np.cos(angle), np.cos(angle)]))
    put("sin", np.concatenate([-np.sin(angle), np.sin(angle)]))
    put("rev", (EXP - np.arange(EXP))[None, :])
    put("token", i[:, None] + P * np.arange(TILES)[None, :])
    t[0:3, CONSTS["sum_parts"][0]:CONSTS["sum_parts"][0] + 2] = [[1, 0], [1, 0], [0, 1]]
    put("thr", np.tile(CHUNK * (1 + np.arange(MAXC)), EXP)[None, :])
    put("expert", np.repeat(np.arange(EXP), MAXC)[None, :])
    put("nth", np.repeat(1 + np.arange(MORE), EXP * MAXC)[None, :])
    return t


def build(nc, xT, wT, uvT, owT, gateT, expw, cols_d, rows_d, embed_rows_d, biasT_d, b2_d, const_d, out):
    ctx = ExitStack()
    with ctx:
        def sb(name, shape, dt=F32):
            return ctx.enter_context(nc.sbuf_tensor(name, shape, dt))

        def sem(name):
            return ctx.enter_context(nc.semaphore(name))

        bank = [ctx.enter_context(nc.psum_tensor(f"bank{i}", [P, 512], F32)) for i in range(8)]

        slots = sb("slots", [P, SLOTS, WCOLS])
        w_emb = slots[:, SLOTS - 2, 0:FK * H].rearrange("p (k n) -> p k n", k=FK)
        w_uv = slots[:, SLOTS - 2, FK * H:FK * H + HK * UV].rearrange("p (k n) -> p k n", k=HK)
        x_in = slots[:, SLOTS - 1, 0:FK * N].rearrange("p (k n) -> p k n", k=FK)
        w_o = slots[:, SLOTS - 1, FK * N:FK * N + EK * H].rearrange("p (k n) -> p k n", k=EK)

        def w1(slot):
            return slots[:, slot, 0:HK * DFF].rearrange("p (k n) -> p k n", k=HK)

        def w2(slot):
            return slots[:, slot, HK * DFF:WCOLS].rearrange("p (k n) -> p k n", k=DK)

        w2_room = sb("w2_room", [P, 2 * 2 * DK * H], F32R)
        w2_parts = w2_room[:, :].rearrange("p (b a k n) -> p b a k n", b=2, a=2, k=DK)
        uv_at, xn_at = HK * UV, 2 * HK * UV
        uv_hi = w2_room[:, 0:uv_at].rearrange("p (k n) -> p k n", k=HK)
        uv_lo = w2_room[:, uv_at:xn_at].rearrange("p (k n) -> p k n", k=HK)
        xnT_hi = w2_room[:, xn_at:xn_at + HK * N].rearrange("p (k n) -> p k n", k=HK)
        xnT_lo = w2_room[:, xn_at + HK * N:xn_at + 2 * HK * N].rearrange("p (k n) -> p k n", k=HK)
        u_parts = w2_room[:, 2 * DK * H:].rearrange("p (a m n) -> p a m n", a=2, m=EK)
        hid_room = sb("hid_room", [P, 2 * 2 * DK * CHUNK], F32R)
        hid_parts = hid_room[:, :].rearrange("p (b a k c) -> p b a k c", b=2, a=2, k=DK)
        wo_parts = hid_room[:, 2 * TILES * H:].rearrange("p (a m n) -> p a m n", a=2, m=EK)
        h2_hi = hid_room[:, 0:TILES * H].rearrange("p (t h) -> p t h", t=TILES)
        h2_lo = hid_room[:, TILES * H:2 * TILES * H].rearrange("p (t h) -> p t h", t=TILES)
        onehot = hid_room[:, 2 * TILES * H:2 * TILES * H + (TILES + 2) * HALF]\
            .rearrange("p (b n) -> p b n", b=TILES + 2)

        cols = sb("cols", [P, NCOLS])
        embed_rows = sb("embed_rows", [TOK + 1, H + P])
        pos_and_b, token_pos = embed_rows[:, 0:H], embed_rows[:, H:]
        pos = sb("pos", [P, H])
        rows = sb("rows", [P, H + E_DIM])
        o_b, v_b = rows[:, 0:H], rows[:, H:]
        slot_rows = rows[0:3, 0:N + CHUNK]
        rel_bias = sb("rel_bias", [P, P])
        gate = sb("gate", [P, HK, EXP])
        const = sb("const", [P, NCONSTS])

        def col(name, i=0, n=1):
            return cols[:, COLS[name][0] + i:COLS[name][0] + i + n]

        def con(name, rows_=P):
            a, n = CONSTS[name]
            return const[0:rows_, a:a + n]

        ident = con("ident")
        iota = sb("iota", [P, N])
        upper = sb("upper", [P, P], BF16)
        ones = sb("ones", [P, P], BF16)
        minus_half = sb("minus_half", [P, 1])
        warm = sb("warm", [P, 1])

        xs = sb("xs", [P, HK, N + CHUNK])
        z = sb("z", [P, TILES, H])
        h2 = z
        xn = sb("xn", [P, TILES, H])
        h2T = xn[:, :, :].rearrange("p t (k n) -> p t k n", k=HK)
        uT = sb("uT", [P, EK, N])
        xnT = uT[:, 0:HK, :]
        h = uT[:, HK:, :].rearrange("p a n -> p (a n)").rearrange("p (t h) -> p t h", t=TILES)
        v = sb("v", [P, TILES, E_DIM])
        hid = v[:, :, :].rearrange("p t e -> p (t e)").rearrange("p (b k c) -> p b k c", b=2, k=DK)
        rotary = sb("rotary", [P, 6, N])
        base = rotary[:, 0:2, :]
        qk = rotary[:, 2:4, :]
        qk_sw = rotary[:, 4:6, :]
        b2 = rotary[:, 0:4, :].rearrange("p a n -> p (a n)").rearrange("p (e h) -> p e h", e=EXP)
        yc = rotary[:, 4, :].rearrange("p (b h) -> p b h", b=2)
        result = rotary[:, 5, :].rearrange("p (b h) -> p b h", b=2)
        att = sb("att", [P, TILES, P])
        xc = sb("xc", [P, 2, HK, CHUNK])
        rows_c = sb("rows_c", [3, 2, CHUNK], F32R)
        sum_parts = sb("sum_parts", [3, 2], F32R)
        wt = sb("wt", [P, 2, 2])
        token_u = sb("token_u", [P, 2], U32)
        b1_more = sb("b1_more", [P, MORE, DK])
        b2_more = uT[:, 0:2, :].rearrange("p a n -> p (a n)")[:, 0:MORE * H].rearrange("p (m h) -> p m h", m=MORE)
        LNS = 2 * TILES + EXP + MORE
        stats = sb("stats", [P, LNS, 6])
        mv = sb("mv", [P, LNS, 2])
        vare = sb("vare", [P, LNS])
        rstd = sb("rstd", [P, LNS])
        logit = sb("logit", [P, TILES, EXP])
        top = sb("top", [P, TILES])
        ntop = sb("ntop", [P, TILES])
        expl = sb("expl", [P, TILES, EXP])
        expsum = sb("expsum", [P, TILES])
        weight = sb("weight", [P, TILES])
        cand = sb("cand", [P, TILES, EXP])
        first = sb("first", [P, TILES])
        chosen = sb("chosen", [P, TILES, EXP], BF16)
        before = sb("before", [P, TILES, EXP], BF16)
        mine = sb("mine", [P, TILES, EXP])
        slot = sb("slot", [P, TILES])
        parts = sb("parts", [P, TILES, P], F32R)
        offs = sb("offs", [1, EXP])
        zero32 = sb("zero32", [1, EXP * MAXC])
        total = sb("total", [1, EXP])
        over = sb("over", [1, EXP, MAXC])
        place = sb("place", [1, EXP * MAXC])
        from_a = sb("from_a", [1, EXP, MAXC])
        end = sb("end", [1, EXP])
        pick = sb("pick", [1, 1, MORE, EXP * MAXC])
        pick2 = sb("pick2", [1, 2, MORE, EXP * MAXC])
        meta_f = sb("meta_f", [1, 16])
        meta = sb("meta", [1, 16], I32)
        M_MORE, M_EXPERT, M_FROM = EXP, EXP + 1, EXP + 1 + MORE

        in_x = [sem(f"in_x{k}") for k in range(FK)]
        in_const = sem("in_const")
        in_cols = sem("in_cols")
        in_bias = sem("in_bias")
        in_rows = sem("in_rows")
        in_uv = sem("in_uv")
        in_u = sem("in_u")
        in_embed_rows = sem("in_embed_rows")
        in_ow = sem("in_ow")
        in_gate = sem("in_gate")
        in_b2 = sem("in_b2")
        in_w = [sem(f"in_w{i}") for i in range(SLOTS)]
        made_const = sem("made_const")
        warmed = sem("warmed")
        pos_done = sem("pos_done")
        pos_ready = sem("pos_ready")
        emb_done = sem("emb_done")
        h_ready = sem("h_ready")
        z0_ready = sem("z0_ready")
        stats_done = sem("stats_done")
        mv_ready = sem("mv_ready")
        vare_ready = sem("vare_ready")
        rstd_ready = sem("rstd_ready")
        xn_ready = sem("xn_ready")
        xnT_done = sem("xnT_done")
        xnT_ready = sem("xnT_ready")
        v_done = sem("v_done")
        vpre_ready = sem("vpre_ready")
        v_ready = sem("v_ready")
        base_done = sem("base_done")
        base_ready = sem("base_ready")
        affine_a = sem("affine_a")
        affine_d = sem("affine_d")
        rope_a = sem("rope_a")
        rope_b = sem("rope_b")
        rope_p = sem("rope_p")
        qk_ready = sem("qk_ready")
        u_done = sem("u_done")
        u_ready = sem("u_ready")
        score_done = sem("score_done")
        biased = sem("biased")
        clipped = sem("clipped")
        att_ready = sem("att_ready")
        av_done = sem("av_done")
        gated = sem("gated")
        o_done = sem("o_done")
        z_ready = sem("z_ready")
        h2_ready = sem("h2_ready")
        h2T_done = sem("h2T_done")
        h2T_ready = sem("h2T_ready")
        logit_done = sem("logit_done")
        route = sem("route")
        ntop_ready = sem("ntop_ready")
        split_hi = sem("split_hi")
        split_lo = sem("split_lo")
        weight_hi = sem("weight_hi")
        parts_ready = sem("parts_ready")
        zeroed = sem("zeroed")
        rows_ready = sem("rows_ready")
        onehot_used = sem("onehot_used")
        exp_ready = sem("exp_ready")
        chosen_ready = sem("chosen_ready")
        rank_done = sem("rank_done")
        onehot_ready = sem("onehot_ready")
        meta_ready = sem("meta_ready")
        sort_done = sem("sort_done")
        xs_ready = sem("xs_ready")
        xc_ready = sem("xc_ready")
        rows_c_ready = sem("rows_c_ready")
        hid_done = sem("hid_done")
        hid_raw = sem("hid_raw")
        hid_hi = sem("hid_hi")
        hid_lo = sem("hid_lo")
        w2_hi = sem("w2_hi")
        w2_lo_d = sem("w2_lo_d")
        w2_lo_p = sem("w2_lo_p")
        uv_hi_ready = sem("uv_hi_ready")
        uv_lo_d = sem("uv_lo_d")
        uv_lo_p = sem("uv_lo_p")
        wo_hi = sem("wo_hi")
        wo_lo = sem("wo_lo")
        gated_hi = sem("gated_hi")
        gated_lo = sem("gated_lo")
        xnT_hi_ready = sem("xnT_hi_ready")
        xnT_lo_p = sem("xnT_lo_p")
        xnT_lo_d = sem("xnT_lo_d")
        b_more = sem("b_more")
        yc_done = sem("yc_done")
        turned = sem("turned")
        wt_ready = sem("wt_ready")
        token_ready = sem("token_ready")
        rest_ready = sem("rest_ready")
        mixed = sem("mixed")
        result_ready = sem("result_ready")
        out_stored = sem("out_stored")

        block = ctx.enter_context(nc.Block())

        def tile(t):
            return slice(t * P, (t + 1) * P)

        def emb_bank(t):
            return bank[(0, 1, 6, 7)[t]][:, 0:H]

        pos_bank = bank[2][:, 0:H]

        def xnT_bank(t):
            return bank[2 + t % 2][:, 0:H].rearrange("p (k n) -> p k n", k=HK)

        def v_bank(t):
            return bank[(4, 5, 0, 1)[t]][:, :]

        base_bank = bank[6]

        def u_bank(m):
            return bank[(7, 2, 3, 0)[m]][:, :]

        def score_bank(t):
            return bank[(5, 5, 6, 6)[t]][:, (t % 2) * P:(t % 2 + 1) * P]

        def av_bank(t):
            return bank[(4, 5, 3, 6)[t]][:, :]

        def o_bank(t):
            return bank[(0, 1, 7, 2)[t]][:, 0:H]

        def h2T_bank(t):
            return bank[(3, 6, 0, 1)[t]][:, 0:H].rearrange("p (k n) -> p k n", k=HK)

        logit_bank = bank[4][:, 0:TILES * EXP]
        place_bank = bank[5][:, 0:(TILES + 2) * EXP]

        def sort_bank(half, m):
            return bank[((6, 7), (2, 3))[half][m]][:, 0:HALF]

        def onehot_of(half, t):
            return onehot[:, (half * TILES + t) % (TILES + 2), :]

        rows_bank = bank[4]

        def hid_bank(n, half):
            return bank[(0, 1, 2, 3)[2 * (n % 2) + half]]

        def yc_bank(n):
            return bank[4 + n % 2][:, 0:H]

        def token_bank(n):
            return bank[6 + n % 2][:, 0:H + 2]

        def over_images(name):
            return con(name).unsqueeze(1).to_broadcast([P, IMAGES, TOK])

        def by_image(ap):
            return ap.rearrange("p (i t) -> p i t", i=IMAGES)

        @block.sync
        def _(sp):
            for k in range(FK):
                sp.dma_start(x_in[:, k, :], xT[:, k, :]).then_inc(in_x[k], 16)
                if k == 0:
                    sp.dma_start(embed_rows[:, :], embed_rows_d).then_inc(in_embed_rows, 16)
            sp.wait_ge(in_uv, 16)
            sp.dma_start(w_uv[:, :, 0:E_DIM], uvT[:, :, 0:E_DIM]).then_inc(in_u, 16)
            sp.dma_start(w_o, owT).then_inc(in_ow, 16)
            sp.wait_ge(in_gate, 16)
            sp.wait_ge(in_bias, 16)
            for e in range(SLOTS - 2):
                sp.dma_start(slots[:, e, :], expw[e]).then_inc(in_w[e], 16)
            sp.wait_ge(emb_done, TILES)
            sp.wait_ge(uv_hi_ready, 2)
            sp.wait_ge(uv_lo_d, 1 + HK)
            sp.wait_ge(uv_lo_p, 1)
            sp.dma_start(slots[:, SLOTS - 2, :], expw[SLOTS - 2]).then_inc(in_w[SLOTS - 2], 16)
            sp.wait_ge(score_done, TILES)
            sp.dma_start(rotary[:, 0:4, :].rearrange("p a n -> p (a n)"), b2_d.partition_broadcast(P))\
                .then_inc(in_b2, 16)
            sp.wait_ge(wo_lo, 1)
            sp.dma_start(slots[:, SLOTS - 1, :], expw[SLOTS - 1]).then_inc(in_w[SLOTS - 1], 16)

            def slot_free(n):
                sp.wait_ge(hid_done, 2 * (n - SLOTS) + 2)
                sp.wait_ge(w2_lo_d, n - SLOTS + 1)
                sp.wait_ge(w2_lo_p, n - SLOTS + 1)

            for e in range(SLOTS, EXP):
                slot_free(e)
                sp.dma_start(slots[:, e % SLOTS, :], expw[e]).then_inc(in_w[e % SLOTS], 16)
            sp.wait_ge(meta_ready, 1)
            more = sp.value_load(meta[0:1, M_MORE:M_MORE + 1], min_val=0, max_val=MORE)
            for m in range(MORE):
                with sp.If(more > m):
                    e = sp.value_load(meta[0:1, M_EXPERT + m:M_EXPERT + m + 1], min_val=0, max_val=EXP - 1)
                    slot_free(EXP + m)
                    i = (EXP + m) % SLOTS
                    sp.dma_start(slots[:, i, :], expw[bass.ds(e, 1)].rearrange("a p n -> (a p) n"))\
                        .then_inc(in_w[i], 16)

        @block.gpsimd
        def _(pool):
            pool.memset(ones[:, :], 1.0).then_inc(made_const, 1)
            pool.memset(minus_half[:, :], -0.5).then_inc(made_const, 1)
            pool.memset(zero32[:, :], 0.0).then_inc(made_const, 1)
            pool.memset(parts[:, :, :].bitcast(F32), 0.0).then_inc(made_const, 1)
            pool.wait_ge(made_const, 4)
            pool.affine_select(out=upper[:, :], in_=ones[:, :], compare_op=ALU.is_gt, fill=0.0, base=0,
                               pattern=[[1, P]], channel_multiplier=-1).then_inc(made_const, 1)
            pool.iota(iota[:, :], [[1, N]], base=0, channel_multiplier=0,
                      allow_small_or_imprecise_dtypes=True).then_inc(made_const, 1)

            def rsqrt(i):
                pool.wait_ge(vare_ready, i + 1)
                pool.tensor_tensor(rstd[:, i:i + 1], vare[:, i:i + 1], minus_half[:, :], ALU.pow)\
                    .then_inc(rstd_ready, 1)

            rsqrt(0)
            pool.wait_ge(in_uv, 16)
            pool.wait_ge(uv_hi_ready, 1)
            pool.tensor_tensor(uv_lo[:, 1, E_DIM:], w_uv[:, 1, E_DIM:], uv_hi[:, 1, E_DIM:].bitcast(F32), ALU.subtract)\
                .then_inc(uv_lo_p, 1)

            def lower_xnT(t):
                pool.wait_ge(xnT_hi_ready, t + 1)
                pool.tensor_tensor(xnT_lo[:, :, tile(t)], xnT[:, :, tile(t)], xnT_hi[:, :, tile(t)].bitcast(F32),
                                   ALU.subtract).then_inc(xnT_lo_p, 1)

            rsqrt(1)
            lower_xnT(0)
            rsqrt(2)
            lower_xnT(1)
            rsqrt(3)

            def start_z(t):
                pool.wait_ge(h_ready, t + 1)
                pool.tensor_tensor(z[:, t, :], h[:, t, :], h[:, t, :], ALU.add).then_inc(z0_ready, 1)
                pool.wait_ge(z0_ready, 2 * t + 1)
                pool.tensor_tensor(z[:, t, :], z[:, t, :], o_b, ALU.add).then_inc(z0_ready, 1)

            pool.wait_ge(in_rows, 16)
            start_z(0)
            start_z(1)
            pool.wait_ge(in_const, 16)
            pool.wait_ge(affine_a, 1)
            pool.tensor_tensor(by_image(qk_sw[:, 0, :]), by_image(qk_sw[:, 0, :]), over_images("sin"), ALU.mult)\
                .then_inc(rope_p, 1)
            start_z(2)
            start_z(3)
            pool.memset(xs[:, :, N:], 0.0).then_inc(zeroed, 1)
            pool.wait_ge(wo_hi, 1)
            pool.wait_ge(in_ow, 16)
            pool.tensor_tensor(wo_parts[:, 1, :, :], w_o, wo_parts[:, 0, :, :].bitcast(F32), ALU.subtract)\
                .then_inc(wo_lo, 1)
            pool.wait_ge(z0_ready, 2 * TILES)
            pool.wait_ge(vpre_ready, TILES)
            pool.memset(slot_rows[:, N:], float(2 * N)).then_inc(zeroed, 1)

            for t in range(TILES):
                pool.wait_ge(gated_hi, t + 1)
                pool.tensor_tensor(u_parts[:, 1, :, tile(t)], uT[:, :, tile(t)], u_parts[:, 0, :, tile(t)].bitcast(F32),
                                   ALU.subtract).then_inc(gated_lo, 1)

            def split_w2(n):
                pool.wait_ge(w2_hi, 2 * n + 1)
                pool.tensor_tensor(w2_parts[:, n % 2, 1, DVE_K:, :], w2(n % SLOTS)[:, DVE_K:, :],
                                   w2_parts[:, n % 2, 0, DVE_K:, :].bitcast(F32), ALU.subtract).then_inc(w2_lo_p, 1)

            for t in range(TILES):
                rsqrt(TILES + t)
            split_w2(0)
            split_w2(1)

            def store(n):
                rsqrt(2 * TILES + n)
                pool.wait_ge(result_ready, n + 1)
                pool.wait_ge(token_ready, n + 1)
                if n:
                    pool.wait_ge(out_stored, 16 * n)
                pool.indirect_dma_start(out, bass.IndirectOffsetOnAxis(ap=token_u[:, n % 2:n % 2 + 1], axis=0),
                                        result[:, n % 2, :], None, bounds_check=N - 1, oob_is_err=False)\
                    .then_inc(out_stored, 16)

            for n in range(EXP - 2):
                store(n)
                split_w2(n + 2)
            pool.wait_ge(meta_ready, 1)
            more = pool.value_load(meta[0:1, M_MORE:M_MORE + 1], min_val=0, max_val=MORE)
            for n in range(EXP - 2, EXP + MORE):
                if n + 2 < EXP + MORE:
                    with pool.If(more > n + 2 - EXP):
                        split_w2(n + 2)
                if n < EXP:
                    store(n)
                else:
                    with pool.If(more > n - EXP):
                        store(n)
            pool.wait_ge(out_stored, 16 * EXP)
            for m in range(MORE):
                with pool.If(more > m):
                    pool.wait_ge(out_stored, 16 * (EXP + m + 1))

        @block.scalar
        def _(act):
            for k in range(FK):
                act.dma_start(w_emb[:, k, :], wT[:, k, :]).then_inc(in_x[k], 16)
            act.dma_start(const[:, :], const_d).then_inc(in_const, 16)
            act.dma_start(cols[:, :], cols_d).then_inc(in_cols, 16)
            act.dma_start(w_uv[:, :, E_DIM:], uvT[:, :, E_DIM:]).then_inc(in_uv, 16)
            act.dma_start(rows[:, :], rows_d.partition_broadcast(P)).then_inc(in_rows, 16)
            act.dma_start(rel_bias[:, :], biasT_d).then_inc(in_bias, 16)
            act.dma_start(gate[:, :, :], gateT).then_inc(in_gate, 16)

            act.wait_ge(made_const, 2)
            act.activation(warm[:, :], minus_half[:, :], ACT.Silu).then_inc(warmed, 1)

            def upper_uv(of, arrived):
                act.wait_ge(arrived, 16)
                act.activation(uv_hi[:, :, of], w_uv[:, :, of], ACT.Copy).then_inc(uv_hi_ready, 1)

            def xnT_copy(t):
                act.wait_ge(xnT_done, t + 1)
                for m in range(HK):
                    act.activation(xnT[:, m, tile(t)], xnT_bank(t)[:, m, :], ACT.Identity,
                                   scale=col("ln_w", m), bias=col("ln_b", m)).then_inc(xnT_ready, 1)
                act.wait_ge(xnT_ready, HK * (t + 1))
                act.activation(xnT_hi[:, :, tile(t)], xnT[:, :, tile(t)], ACT.Copy).then_inc(xnT_hi_ready, 1)

            def v_silu(t):
                act.wait_ge(vpre_ready, t + 1)
                act.activation(v[:, t, :], v[:, t, :], ACT.Silu).then_inc(v_ready, 1)

            upper_uv(slice(E_DIM, UV), in_uv)
            act.wait_ge(in_cols, 16)
            xnT_copy(0)
            xnT_copy(1)
            xnT_copy(2)
            xnT_copy(3)
            upper_uv(slice(0, E_DIM), in_u)
            act.wait_ge(in_ow, 16)
            act.activation(wo_parts[:, 0, :, :], w_o, ACT.Copy).then_inc(wo_hi, 1)
            act.wait_ge(base_done, 1)
            act.activation(base[:, 0, :], base_bank[:, :], ACT.Silu, bias=col("base_b")).then_inc(base_ready, 1)
            for a, b in ((0, S // 2), (S // 2, 0)):
                act.activation(base[b:b + S // 2, 1, :], base_bank[a:a + S // 2, :], ACT.Silu,
                               bias=cols[a:a + S // 2, COLS["base_b"][0]:COLS["base_b"][0] + 1]).then_inc(base_ready, 1)
            act.wait_ge(base_ready, 3)
            for j in range(2):
                act.activation(qk_sw[:, j, :], base[:, 1, :], ACT.Identity, scale=col("gamma_sw", j),
                               bias=col("beta_sw", j)).then_inc(affine_a, 1)

            def u_silu(m):
                act.wait_ge(u_done, m + 1)
                act.activation(uT[:, m, :], u_bank(m), ACT.Silu, bias=col("u_b", m)).then_inc(u_ready, 1)

            v_silu(0)
            v_silu(1)
            u_silu(0)
            u_silu(1)
            act.wait_ge(z0_ready, 2 * TILES)
            u_silu(2)
            v_silu(2)
            v_silu(3)
            u_silu(3)

            def split_w2(n):
                act.wait_ge(in_w[n % SLOTS], 16 * (n // SLOTS + 1))
                if n == 0:
                    act.wait_ge(u_done, EK)
                elif n == 1:
                    act.wait_ge(o_done, TILES)
                else:
                    act.wait_ge(yc_done, n - 1)
                for blocks in (slice(DVE_K, DK), slice(0, DVE_K)):
                    act.activation(w2_parts[:, n % 2, 0, blocks, :], w2(n % SLOTS)[:, blocks, :], ACT.Copy)\
                        .then_inc(w2_hi, 1)

            for t in range(TILES):
                act.wait_ge(gated, t + 1)
                act.activation(u_parts[:, 0, :, tile(t)], uT[:, :, tile(t)], ACT.Copy).then_inc(gated_hi, 1)
            split_w2(0)
            for t in range(TILES):
                act.wait_ge(h2T_done, t + 1)
                act.activation(h2T[:, t, :, :], h2T_bank(t), ACT.Copy).then_inc(h2T_ready, 1)
                act.activation(h2_hi[:, t, :], h2[:, t, :], ACT.Copy).then_inc(split_hi, 1)
            split_w2(1)
            for t in range(TILES):
                act.wait_ge(ntop_ready, 1)
                act.activation(expl[:, t, :], logit[:, t, :], ACT.Exp, bias=ntop[:, t:t + 1],
                               accum_out=expsum[:, t:t + 1]).then_inc(exp_ready, 1)
            act.wait_ge(sort_done, 1)
            act.activation(xc[:, 0, 0, :], sort_bank(0, 0)[:, 0:CHUNK], ACT.Copy).then_inc(xc_ready, 1)
            act.activation(xs[:, 0, 0:HALF], sort_bank(0, 0), ACT.Copy).then_inc(xs_ready, 1)
            act.wait_ge(sort_done, HK + 1)
            act.activation(xs[:, 0, HALF:N], sort_bank(1, 0), ACT.Copy).then_inc(xs_ready, 1)

            def hidden(n, b1_col):
                if n >= 2:
                    act.wait_ge(hid_lo, 2 * (n - 1))
                    act.wait_ge(yc_done, n - 1)
                for half in range(2):
                    act.wait_ge(hid_done, 2 * n + half + 1)
                    for c in range(DK // 2):
                        act.activation(hid[:, n % 2, half * DK // 2 + c, :],
                                       hid_bank(n, half)[:, c * CHUNK:(c + 1) * CHUNK], ACT.Relu,
                                       bias=b1_col(half * DK // 2 + c)).then_inc(hid_raw, 1)
                    act.wait_ge(hid_raw, DK * n + (half + 1) * DK // 2)
                    blocks = slice(half * DK // 2, (half + 1) * DK // 2)
                    act.activation(hid_parts[:, n % 2, 0, blocks, :], hid[:, n % 2, blocks, :], ACT.Copy)\
                        .then_inc(hid_hi, 1)

            for n in range(EXP):
                hidden(n, lambda c, n=n: col("b1", n * DK + c))
                if 1 <= n < EXP - 1:
                    split_w2(n + 1)
            act.wait_ge(meta_ready, 1)
            more = act.value_load(meta[0:1, M_MORE:M_MORE + 1], min_val=0, max_val=MORE)
            with act.If(more > 0):
                split_w2(EXP)
            for m in range(MORE):
                with act.If(more > m):
                    act.wait_ge(b_more, 2 * m + 2)
                    hidden(EXP + m, lambda c, m=m: b1_more[:, m, c:c + 1])
                if m + 1 < MORE:
                    with act.If(more > m + 1):
                        split_w2(EXP + m + 1)

        @block.tensor
        def _(pe):
            def embed(t, k):
                mm = pe.matmul(emb_bank(t), x_in[:, k, tile(t)], w_emb[:, k, :], start=(k == 0), stop=(k == FK - 1))
                if k == FK - 1:
                    mm.then_inc(emb_done, 1)

            def keep_busy(times, free):
                for _ in range(times):
                    pe.matmul(free[:, :], ones[:, :], ones[:, :].unsqueeze(1).to_broadcast([P, 4, P]), start=True,
                              stop=True)

            pe.wait_ge(made_const, 1)
            keep_busy(WARMUP, bank[5])
            for k in range(PHASE_K):
                pe.wait_ge(in_x[k], 32)
                for t in range(TILES):
                    embed(t, k)
                if k == 0:
                    pe.wait_ge(in_embed_rows, 16)
                    pe.matmul(pos_bank, token_pos, pos_and_b, start=True, stop=True).then_inc(pos_done, 1)

            def rest_of_embedding(t):
                for k in range(PHASE_K, FK):
                    if t == 0:
                        pe.wait_ge(in_x[k], 32)
                    embed(t, k)

            def products(to, terms):
                for i, (a, b) in enumerate(terms):
                    mm = pe.matmul(to, a, b, start=(i == 0), stop=(i == len(terms) - 1))
                return mm

            PASSES = ((0, 0), (0, 1), (1, 0))
            xnT_parts, uv_parts = (xnT_hi, xnT_lo), (uv_hi, uv_lo)

            def turn_xn(t):
                pe.wait_ge(xn_ready, t + 1)
                if t == 0:
                    pe.wait_ge(in_const, 16)
                if t >= 2:
                    pe.wait_ge(xnT_ready, HK * (t - 1))
                for m in range(HK):
                    tr = pe.transpose(xnT_bank(t)[:, m, :], xn[:, t, tile(m)], ident)
                tr.then_inc(xnT_done, 1)

            def v_product(t):
                pe.wait_ge(xnT_hi_ready, t + 1)
                pe.wait_ge(xnT_lo_p if t < 2 else xnT_lo_d, t % 2 + 1)
                if t == 2:
                    pe.wait_ge(h_ready, TILES)
                products(v_bank(t), [(xnT_parts[a][:, k, tile(t)], uv_parts[b][:, k, E_DIM:2 * E_DIM])
                                     for k in range(HK) for a, b in PASSES]).then_inc(v_done, 1)

            def u_product(m):
                if m == 3:
                    pe.wait_ge(vpre_ready, TILES)
                products(u_bank(m), [(uv_parts[a][:, k, m * P:(m + 1) * P], xnT_parts[b][:, k, :])
                                     for k in range(HK) for a, b in PASSES]).then_inc(u_done, 1)

            rest_of_embedding(0)
            rest_of_embedding(1)
            rest_of_embedding(2)
            turn_xn(0)
            rest_of_embedding(3)
            turn_xn(1)
            pe.wait_ge(uv_hi_ready, 1)
            pe.wait_ge(uv_lo_d, 1)
            pe.wait_ge(uv_lo_p, 1)
            v_product(0)
            turn_xn(2)
            v_product(1)
            turn_xn(3)
            v_product(2)
            pe.wait_ge(xnT_lo_p, 2)
            pe.wait_ge(xnT_lo_d, 2)
            products(base_bank[:, :], [(uv_parts[a][:, k, 2 * E_DIM:UV], xnT_parts[b][:, k, :])
                                       for k in range(HK) for a, b in PASSES]).then_inc(base_done, 1)
            v_product(3)
            pe.wait_ge(uv_hi_ready, 2)
            pe.wait_ge(uv_lo_d, 1 + HK)
            u_product(0)
            u_product(1)
            u_product(2)
            pe.wait_ge(qk_ready, 2)
            for t in range(TILES):
                pe.wait_ge(vpre_ready, 2)
                pe.matmul(score_bank(t), qk[:, 1, tile(t)], qk[:, 0, tile(t)], start=True, stop=True)\
                    .then_inc(score_done, 1)
            u_product(3)

            def attend(t):
                pe.wait_ge(att_ready, t + 1)
                pe.wait_ge(v_ready, t + 1)
                if t == 2:
                    pe.wait_ge(u_ready, EK)
                for m in range(EK):
                    mm = pe.matmul(av_bank(t)[:, tile(m)], v[:, t, tile(m)], att[:, t, :], start=True, stop=True)
                mm.then_inc(av_done, 1)

            def project(t):
                pe.wait_ge(gated_hi, t + 1)
                pe.wait_ge(gated_lo, t + 1)
                pe.wait_ge(wo_lo, 1)
                products(o_bank(t), [(u_parts[:, a, m, tile(t)], wo_parts[:, b, m, :])
                                     for m in range(EK) for a, b in PASSES]).then_inc(o_done, 1)

            def turn_h2(t):
                pe.wait_ge(h2_ready, t + 1)
                for m in range(HK):
                    tr = pe.transpose(h2T_bank(t)[:, m, :], h2[:, t, tile(m)], ident)
                tr.then_inc(h2T_done, 1)

            def logits(t):
                pe.wait_ge(h2T_ready, t + 1)
                pe.wait_ge(in_gate, 16)
                for m in range(HK):
                    mm = pe.matmul(logit_bank[:, t * EXP:(t + 1) * EXP], h2T[:, t, m, :], gate[:, m, :],
                                   start=(m == 0), stop=(m == HK - 1))
                mm.then_inc(logit_done, 1)

            for t in range(TILES):
                attend(t)
            project(0)
            project(1)
            project(2)
            turn_h2(0)
            project(3)
            turn_h2(1)
            logits(0)
            keep_busy(4, bank[5])
            turn_h2(2)
            logits(1)
            keep_busy(2, bank[5])
            turn_h2(3)
            logits(2)
            logits(3)
            keep_busy(5, bank[7])

            pe.wait_ge(made_const, 6)
            pe.wait_ge(chosen_ready, 2)
            blocks = TILES + 2
            by_tile = place_bank.rearrange("p (b e) -> p b e", b=blocks)
            for t in range(TILES):
                pe.matmul(by_tile[:, 0:TILES + 1, :], ones[:, :],
                          before[:, t:t + 1, :].to_broadcast([P, TILES + 1, EXP]),
                          start=(t == 0), stop=False, skip_group_check=True)
                pe.matmul(by_tile[:, TILES + 1, :], ones[:, :], chosen[:, t, :], start=False, stop=False,
                          skip_group_check=True)
                if t + 1 < TILES:
                    pe.matmul(by_tile[:, t + 1:TILES, :], ones[:, :],
                              chosen[:, t:t + 1, :].to_broadcast([P, TILES - 1 - t, EXP]),
                              start=False, stop=False, skip_group_check=True)
                last = pe.matmul(by_tile[:, t, :], upper[:, :], chosen[:, t, :], start=False,
                                 stop=(t == TILES - 1), skip_group_check=True)
            last.then_inc(rank_done, 1)
            keep_busy(4, bank[0])

            def sort(half, t):
                pe.wait_ge(onehot_ready, half * TILES + t + 1)
                pe.wait_ge(split_lo, t + 1)
                for m in range(HK):
                    for part in (h2_hi, h2_lo):
                        mm = pe.matmul(sort_bank(half, m), part[:, t, tile(m)], onehot_of(half, t),
                                       start=(t == 0 and part is h2_hi), stop=(t == TILES - 1 and part is h2_lo))
                    if t == TILES - 1:
                        mm.then_inc(sort_done, 1)

            def sort_rows(half, t):
                pe.wait_ge(parts_ready, 2)
                pe.matmul(rows_bank[:, half * HALF:(half + 1) * HALF], parts[:, t, :], onehot_of(half, t),
                          start=(t == 0), stop=(t == TILES - 1)).then_inc(onehot_used, 1)

            for t in range(TILES):
                sort(0, t)
            for t in range(TILES):
                sort_rows(0, t)
            for t in range(TILES):
                sort(1, t)
                sort_rows(1, t)

            def hidden(n, slot_):
                pe.wait_ge(xc_ready, n + 2)
                if n >= 2:
                    pe.wait_ge(hid_raw, DK * (n - 1))
                for c in range(DK):
                    for k in range(HK):
                        mm = pe.matmul(hid_bank(n, c // 4)[:, (c % 4) * CHUNK:(c % 4 + 1) * CHUNK],
                                       w1(slot_)[:, k, c * P:(c + 1) * P], xc[:, n % 2, k, :], start=(k == 0),
                                       stop=(k == HK - 1))
                    if c % 4 == 3:
                        mm.then_inc(hid_done, 1)

            def turn(n):
                if n == 0:
                    pe.wait_ge(xs_ready, 4)
                if n >= 2:
                    pe.wait_ge(rest_ready, n - 1)
                for k in range(HK):
                    pe.transpose(token_bank(n)[:, tile(k)], xc[:, n % 2, k, :], ident)
                pe.wait_ge(rows_c_ready, n + 2)
                pe.matmul(token_bank(n)[:, H:H + 2], rows_c[:, n % 2, :], sum_parts[:, :], start=True, stop=True)\
                    .then_inc(turned, 1)

            def output(n):
                if n == 0:
                    pe.wait_ge(rows_ready, 1)
                if n >= 2:
                    pe.wait_ge(mixed, n - 1)
                pe.wait_ge(w2_hi, 2 * n + 2)
                pe.wait_ge(w2_lo_d, n + 1)
                pe.wait_ge(w2_lo_p, n + 1)
                for c in range(DK):
                    if c % (DK // 2) == 0:
                        half = c // (DK // 2)
                        pe.wait_ge(hid_hi, 2 * n + half + 1)
                        pe.wait_ge(hid_lo, 2 * n + half + 1)
                    for i, (a, b) in enumerate(PASSES):
                        mm = pe.matmul(yc_bank(n), hid_parts[:, n % 2, a, c, :], w2_parts[:, n % 2, b, c, :],
                                       start=(c == 0 and i == 0), stop=(c == DK - 1 and i == len(PASSES) - 1))
                mm.then_inc(yc_done, 1)

            for n in range(EXP):
                if n == EXP - 1:
                    pe.wait_ge(meta_ready, 1)
                    more = pe.value_load(meta[0:1, M_MORE:M_MORE + 1], min_val=0, max_val=MORE)
                pe.wait_ge(in_w[n % SLOTS], 16 * (n // SLOTS + 1))
                hidden(n, n % SLOTS)
                turn(n)
                if n:
                    output(n - 1)
            for m in range(MORE):
                with pe.If(more > m):
                    pe.wait_ge(in_w[(EXP + m) % SLOTS], 16 * ((EXP + m) // SLOTS + 1))
                    hidden(EXP + m, (EXP + m) % SLOTS)
                    turn(EXP + m)
                if m == 0:
                    output(EXP - 1)
                else:
                    with pe.If(more > m - 1):
                        output(EXP + m - 1)
            with pe.If(more > MORE - 1):
                output(EXP + MORE - 1)

        @block.vector
        def _(dve):
            def moments(i, src):
                first_moments(i, src)
                last_moments(i)

            def first_moments(i, src):
                dve.bn_stats(stats[:, i, :], src).then_inc(stats_done, 1)

            def last_moments(i):
                dve.wait_ge(stats_done, i + 1)
                dve.bn_aggr(mv[:, i, :], stats[:, i, :]).then_inc(mv_ready, 1)
                dve.wait_ge(mv_ready, i + 1)
                dve.tensor_scalar(vare[:, i:i + 1], mv[:, i, 1:2], EPS, None, ALU.add).then_inc(vare_ready, 1)

            def normalise(i, dst, src, done):
                dve.wait_ge(mv_ready, i + 1)
                dve.wait_ge(rstd_ready, i + 1)
                dve.tensor_scalar(dst, src, mv[:, i, 0:1], rstd[:, i:i + 1], ALU.subtract, ALU.mult).then_inc(done, 1)

            def lower_uv(part, k, of, arrived):
                dve.wait_ge(arrived, 16)
                dve.wait_ge(uv_hi_ready, part + 1)
                dve.tensor_tensor(uv_lo[:, k, of], w_uv[:, k, of], uv_hi[:, k, of].bitcast(F32), ALU.subtract)\
                    .then_inc(uv_lo_d, 1)

            dve.wait_ge(pos_done, 1)
            dve.tensor_copy(pos[:, :], pos_bank).then_inc(pos_ready, 1)
            dve.wait_ge(pos_ready, 1)

            def add_pos(t):
                dve.wait_ge(emb_done, t + 1)
                dve.tensor_tensor(h[:, t, :], emb_bank(t), pos[:, :], ALU.add).then_inc(h_ready, 1)

            def moments1(t):
                dve.wait_ge(h_ready, t + 1)
                moments(t, h[:, t, :])

            def norm1(t):
                normalise(t, xn[:, t, :], h[:, t, :], xn_ready)

            add_pos(0)
            moments1(0)
            add_pos(1)
            norm1(0)
            moments1(1)
            add_pos(2)
            lower_uv(0, 0, slice(E_DIM, UV), in_uv)
            norm1(1)
            moments1(2)
            add_pos(3)
            norm1(2)
            moments1(3)
            norm1(3)
            for t in (2, 3):
                dve.wait_ge(xnT_hi_ready, t + 1)
                dve.tensor_tensor(xnT_lo[:, :, tile(t)], xnT[:, :, tile(t)], xnT_hi[:, :, tile(t)].bitcast(F32),
                                  ALU.subtract).then_inc(xnT_lo_d, 1)

            def add_v_b(t):
                dve.wait_ge(v_done, t + 1)
                dve.tensor_tensor(v[:, t, :], v_bank(t), v_b, ALU.add).then_inc(vpre_ready, 1)

            dve.wait_ge(in_rows, 16)
            lower_uv(1, 0, slice(0, E_DIM), in_u)
            lower_uv(1, 1, slice(0, E_DIM), in_u)
            add_v_b(0)

            dve.wait_ge(in_const, 16)
            dve.wait_ge(in_cols, 16)
            dve.wait_ge(base_ready, 1)
            for j in range(2):
                dve.tensor_scalar(qk[:, j, :], base[:, 0, :], col("gamma", j), col("beta", j), ALU.mult, ALU.add)\
                    .then_inc(affine_d, 1)
            for j in range(2):
                dve.wait_ge(affine_d, j + 1)
                dve.tensor_tensor(by_image(qk[:, j, :]), by_image(qk[:, j, :]), over_images("cos"), ALU.mult)\
                    .then_inc(rope_a, 1)
            add_v_b(1)
            dve.wait_ge(affine_a, 2)
            dve.tensor_tensor(by_image(qk_sw[:, 1, :]), by_image(qk_sw[:, 1, :]), over_images("sin"), ALU.mult)\
                .then_inc(rope_b, 1)
            for j in range(2):
                dve.wait_ge(rope_a, j + 1)
                dve.wait_ge(rope_b if j else rope_p, 1)
                dve.tensor_tensor(qk[:, j, :], qk[:, j, :], qk_sw[:, j, :], ALU.add).then_inc(qk_ready, 1)
            add_v_b(2)
            add_v_b(3)

            def attention(t):
                dve.wait_ge(in_bias, 16)
                dve.wait_ge(score_done, 2 * (t // 2) + 2)
                dve.scalar_tensor_tensor(out=att[:, t, :], in0=score_bank(t), scalar=1.0 / float(np.sqrt(S)),
                                         in1=rel_bias[:, :], op0=ALU.mult, op1=ALU.add).then_inc(biased, 1)
                dve.wait_ge(biased, t + 1)
                dve.scalar_tensor_tensor(out=att[:, t, :], in0=att[:, t, :], scalar=0.0, in1=con("block"),
                                         op0=ALU.max, op1=ALU.mult).then_inc(clipped, 1)
                dve.wait_ge(clipped, t + 1)
                dve.tensor_tensor(att[:, t, :], att[:, t, :], att[:, t, :], ALU.mult).then_inc(att_ready, 1)

            def gate_u(t):
                dve.wait_ge(av_done, t + 1)
                dve.wait_ge(u_ready, EK)
                dve.tensor_tensor(uT[:, :, tile(t)], uT[:, :, tile(t)],
                                  av_bank(t).rearrange("p (m n) -> p m n", m=EK), ALU.mult).then_inc(gated, 1)

            def residual(t):
                dve.wait_ge(o_done, t + 1)
                dve.wait_ge(z0_ready, 2 * (t + 1))
                dve.tensor_tensor(z[:, t, :], z[:, t, :], o_bank(t), ALU.add).then_inc(z_ready, 1)
                dve.wait_ge(z_ready, t + 1)
                first_moments(TILES + t, z[:, t, :])

            def norm2(t):
                normalise(TILES + t, h2[:, t, :], z[:, t, :], h2_ready)

            def rest_of_h2(t):
                dve.wait_ge(split_hi, t + 1)
                dve.tensor_tensor(h2_lo[:, t, :], h2[:, t, :], h2_hi[:, t, :].bitcast(F32), ALU.subtract)\
                    .then_inc(split_lo, 1)

            def split_w2(n):
                dve.wait_ge(w2_hi, 2 * n + 2)
                dve.tensor_tensor(w2_parts[:, n % 2, 1, 0:DVE_K, :], w2(n % SLOTS)[:, 0:DVE_K, :],
                                  w2_parts[:, n % 2, 0, 0:DVE_K, :].bitcast(F32), ALU.subtract).then_inc(w2_lo_d, 1)

            attention(0)
            attention(1)
            attention(2)
            gate_u(0)
            attention(3)
            gate_u(1)
            gate_u(2)
            gate_u(3)
            for t in range(TILES):
                residual(t)
                if t:
                    norm2(t - 1)
                last_moments(TILES + t)
            rest_of_h2(0)
            rest_of_h2(1)
            norm2(3)

            step = [0]

            def then(ins):
                step[0] += 1
                ins.then_inc(route, 1)
                dve.wait_ge(route, step[0])

            rest_of_h2(2)
            logits = logit_bank.rearrange("p (t e) -> p t e", t=TILES)
            rev = con("rev").unsqueeze(1).to_broadcast([P, TILES, EXP])

            def per_tile(ap):
                return ap.unsqueeze(2).to_broadcast([P, TILES, EXP])

            dve.wait_ge(logit_done, TILES)
            then(dve.tensor_reduce(top[:, :], logits, AX_X, ALU.max))
            then(dve.tensor_tensor(cand[:, :, :], logits, per_tile(top[:, :]), ALU.is_equal))
            then(dve.tensor_tensor(cand[:, :, :], cand[:, :, :], rev, ALU.mult))
            then(dve.tensor_reduce(first[:, :], cand[:, :, :], AX_X, ALU.max))
            dve.tensor_tensor(before[:, :, :], rev, per_tile(first[:, :]), ALU.is_lt).then_inc(chosen_ready, 1)
            dve.tensor_tensor(chosen[:, :, :], rev, per_tile(first[:, :]), ALU.is_equal).then_inc(chosen_ready, 1)
            then(dve.tensor_copy(logit[:, :, :], logits))
            dve.tensor_scalar(ntop[:, :], top[:, :], -1.0, None, ALU.mult).then_inc(ntop_ready, 1)
            dve.wait_ge(chosen_ready, 2)
            dve.wait_ge(rank_done, 1)
            places = place_bank.rearrange("p (b e) -> p b e", b=TILES + 2)
            then(dve.tensor_tensor(mine[:, :, :], places[:, 0:TILES, :], chosen[:, :, :], ALU.mult))
            then(dve.tensor_reduce(slot[:, :], mine[:, :, :], AX_X, ALU.add))

            dve.wait_ge(made_const, 6)

            def make_onehot(half, t):
                if half and t >= 2:
                    dve.wait_ge(onehot_used, t - 1)
                dve.tensor_scalar(onehot_of(half, t), iota[:, half * HALF:(half + 1) * HALF], slot[:, t:t + 1], None,
                                  ALU.is_equal).then_inc(onehot_ready, 1)

            for t in range(TILES):
                make_onehot(0, t)
            rest_of_h2(3)
            dve.wait_ge(exp_ready, TILES)
            then(dve.reciprocal(weight[:, :], expsum[:, :]))
            dve.tensor_copy(parts[:, :, 0], weight[:, :]).then_inc(weight_hi, 1)
            dve.tensor_copy(parts[:, :, 2], con("token")).then_inc(parts_ready, 1)
            dve.wait_ge(weight_hi, 1)
            dve.tensor_tensor(parts[:, :, 1], weight[:, :], parts[:, :, 0].bitcast(F32), ALU.subtract)\
                .then_inc(parts_ready, 1)
            then(dve.tensor_copy(offs[:, :], places[0:1, TILES, :]))
            then(dve.tensor_copy(total[:, :], places[0:1, TILES + 1, :]))
            then(dve.tensor_copy(meta[:, 0:EXP], offs[:, :]))
            for t in range(TILES):
                make_onehot(1, t)
            dve.wait_ge(sort_done, 2)
            dve.tensor_copy(xc[:, 0, 1, :], sort_bank(0, 1)[:, 0:CHUNK]).then_inc(xc_ready, 1)
            dve.tensor_copy(xs[:, 1, 0:HALF], sort_bank(0, 1)).then_inc(xs_ready, 1)
            split_w2(0)

            dve.wait_ge(sort_done, 2 * HK)
            dve.tensor_copy(xs[:, 1, HALF:N], sort_bank(1, 1)).then_inc(xs_ready, 1)
            dve.wait_ge(zeroed, 2)
            dve.wait_ge(onehot_used, 2 * TILES)
            dve.tensor_copy(slot_rows[:, 0:N], rows_bank[0:3, :]).then_inc(rows_ready, 1)
            dve.wait_ge(rows_ready, 1)
            dve.wait_ge(xs_ready, 4)

            def fetch_chunk(n, at):
                start = dve.value_load(meta[0:1, at:at + 1], min_val=0, max_val=N)
                if n >= 2:
                    dve.wait_ge(hid_done, 2 * (n - 1))
                    dve.wait_ge(turned, n - 1)
                if n:
                    dve.tensor_copy(xc[:, n % 2, :, :], xs[:, :, bass.ds(start, CHUNK)]).then_inc(xc_ready, 1)
                dve.tensor_copy(rows_c[:, n % 2, :], slot_rows[:, bass.ds(start, CHUNK)]).then_inc(rows_c_ready, 1)

            def fetch_more(m):
                fetch_chunk(EXP + m, M_FROM + m)
                e = dve.value_load(meta[0:1, M_EXPERT + m:M_EXPERT + m + 1], min_val=0, max_val=EXP - 1)
                b1_all = col("b1", 0, EXP * DK).rearrange("p (e c) -> p e c", e=EXP)
                dve.tensor_copy(b1_more[:, m:m + 1, :], b1_all[:, bass.ds(e, 1), :]).then_inc(b_more, 1)
                dve.tensor_copy(b2_more[:, m:m + 1, :], b2[:, bass.ds(e, 1), :]).then_inc(b_more, 1)

            def lower_hidden(n, halves=(0, 1)):
                for half in halves:
                    dve.wait_ge(hid_hi, 2 * n + half + 1)
                    blocks = slice(half * DK // 2, (half + 1) * DK // 2)
                    dve.tensor_tensor(hid_parts[:, n % 2, 1, blocks, :], hid[:, n % 2, blocks, :],
                                      hid_parts[:, n % 2, 0, blocks, :].bitcast(F32), ALU.subtract).then_inc(hid_lo, 1)

            def rest(n, b2_row):
                dve.wait_ge(turned, n + 1)
                if n >= 2:
                    dve.wait_ge(out_stored, 16 * (n - 1))
                dve.tensor_copy(wt[:, n % 2, :], token_bank(n)[:, H:H + 2]).then_inc(wt_ready, 1)
                dve.tensor_copy(token_u[:, n % 2:n % 2 + 1], token_bank(n)[:, H + 1:H + 2]).then_inc(token_ready, 1)
                dve.wait_ge(wt_ready, n + 1)
                dve.scalar_tensor_tensor(out=yc[:, n % 2, :], in0=b2_row, scalar=wt[:, n % 2, 0:1],
                                         in1=token_bank(n)[:, 0:H], op0=ALU.mult, op1=ALU.add).then_inc(rest_ready, 1)

            def output_moments(n):
                dve.wait_ge(yc_done, n + 1)
                dve.wait_ge(rest_ready, n + 1)
                dve.scalar_tensor_tensor(out=yc[:, n % 2, :], in0=yc_bank(n), scalar=wt[:, n % 2, 0:1],
                                         in1=yc[:, n % 2, :], op0=ALU.mult, op1=ALU.add).then_inc(mixed, 1)
                dve.wait_ge(mixed, n + 1)
                moments(2 * TILES + n, yc[:, n % 2, :])

            def output(n):
                output_moments(n)
                output_norm(n)

            def output_norm(n):
                normalise(2 * TILES + n, result[:, n % 2, :], yc[:, n % 2, :], result_ready)

            def count_more():
                by_expert = [1, EXP, MAXC]

                def spread(ap):
                    return ap.unsqueeze(2).to_broadcast(by_expert)

                thr = con("thr", 1).rearrange("p (e c) -> p e c", e=EXP)
                then(dve.tensor_tensor(end[:, :], offs[:, :], total[:, :], ALU.add))
                then(dve.tensor_tensor(over[:, :, :], spread(total[:, :]), thr, ALU.is_gt))
                over_row = over[:, :, :].rearrange("p e c -> p (e c)")
                then(dve.tensor_tensor_scan(place[:, :], over_row, zero32[:, :], 0.0, ALU.add, ALU.add))
                then(dve.tensor_copy(meta_f[:, M_MORE:M_MORE + 1], place[:, EXP * MAXC - 1:EXP * MAXC]))
                then(dve.tensor_tensor(place[:, :], place[:, :], over_row, ALU.mult))
                then(dve.tensor_tensor(from_a[:, :, :], spread(offs[:, :]), thr, ALU.add))
                then(dve.tensor_scalar(end[:, :], end[:, :], float(-CHUNK), None, ALU.add))
                then(dve.tensor_tensor(from_a[:, :, :], from_a[:, :, :], spread(end[:, :]), ALU.min))
                nth = con("nth", 1).rearrange("p (m i) -> p m i", m=MORE)

                def for_each(ap):
                    return ap.unsqueeze(1).to_broadcast([1, MORE, EXP * MAXC])

                then(dve.tensor_tensor(pick[:, 0, :, :], for_each(place[:, :]), nth, ALU.is_equal))
                then(dve.tensor_tensor(pick2[:, 0, :, :], pick[:, 0, :, :], for_each(con("expert", 1)), ALU.mult))
                then(dve.tensor_tensor(pick2[:, 1, :, :], pick[:, 0, :, :],
                                       for_each(from_a[:, :, :].rearrange("p e c -> p (e c)")), ALU.mult))
                then(dve.tensor_reduce(meta_f[:, M_EXPERT:M_EXPERT + 2 * MORE],
                                       pick2[:, :, :, :].rearrange("p a m i -> p (a m) i"), AX_X, ALU.add))
                dve.tensor_copy(meta[:, M_MORE:M_MORE + 1 + 2 * MORE], meta_f[:, M_MORE:M_MORE + 1 + 2 * MORE])\
                    .then_inc(meta_ready, 1)
                dve.wait_ge(meta_ready, 1)

            dve.tensor_copy(sum_parts[:, :], con("sum_parts", 3)).then_inc(rows_c_ready, 1)
            dve.wait_ge(in_b2, 16)
            dve.wait_ge(in_cols, 16)
            fetch_chunk(0, 0)
            fetch_chunk(1, 1)
            for n in range(EXP):
                if n:
                    rest(n - 1, b2[:, n - 1, :])
                lower_hidden(n)
                if n == 0:
                    split_w2(1)
                if n == EXP - 2:
                    more = dve.value_load(meta[0:1, M_MORE:M_MORE + 1], min_val=0, max_val=MORE)
                if n + 2 < EXP:
                    fetch_chunk(n + 2, n + 2)
                else:
                    with dve.If(more > n + 2 - EXP):
                        fetch_more(n + 2 - EXP)
                if n == EXP - 1:
                    with dve.If(more > 0):
                        split_w2(EXP)
                if n == EXP - 1:
                    output_moments(n - 1)
                    with dve.If(more > 0):
                        lower_hidden(EXP, (0,))
                    output_norm(n - 1)
                elif n:
                    output(n - 1)
                    split_w2(n + 1)
                if n == 1:
                    count_more()
            for m in range(MORE):
                with dve.If(more > m):
                    lower_hidden(EXP + m, (1,) if m == 0 else (0, 1))
                if m == 0:
                    rest(EXP - 1, b2[:, EXP - 1, :])
                if m + 2 < MORE:
                    with dve.If(more > m + 2):
                        fetch_more(m + 2)
                if m + 1 < MORE:
                    with dve.If(more > m + 1):
                        split_w2(EXP + m + 1)
                if m == 0:
                    output(EXP - 1)
                else:
                    with dve.If(more > m - 1):
                        output(EXP + m - 1)
                with dve.If(more > m):
                    rest(EXP + m, b2_more[:, m, :])
            with dve.If(more > MORE - 1):
                output(EXP + MORE - 1)


def kernel(x, L0_tok_W, L0_tok_b, L0_tok_pos_emb, L0_attn_ln_w, L0_attn_ln_b, L0_attn_uv_w, L0_attn_uv_b,
           L0_attn_gamma, L0_attn_beta, L0_attn_w, L0_attn_o_w, L0_attn_o_b, L0_ffn_gate_w, L0_ffn_w1, L0_ffn_b1,
           L0_ffn_w2, L0_ffn_b2):
    import concourse.bacc as bacc
    from concourse.bass_utils import run_bass_kernel_spmd

    def chunks(a):
        a = np.asarray(a)
        return np.ascontiguousarray(a.reshape(a.shape[0] // P, P, a.shape[1]).transpose(1, 0, 2))

    def column(a):
        return np.asarray(a).reshape(-1, P).T

    def swap(a):
        return np.concatenate([a[S // 2:], a[:S // 2]])

    patches = np.asarray(x).reshape(IMAGES, CH, SIDE, PATCH, SIDE, PATCH).transpose(0, 2, 4, 1, 3, 5).reshape(N, FEAT)
    uv_b = np.asarray(L0_attn_uv_b)
    gamma, beta = np.asarray(L0_attn_gamma).T, np.asarray(L0_attn_beta).T
    base_b = uv_b[2 * E_DIM:].reshape(S, 1)
    cols = {"ln_w": column(L0_attn_ln_w), "ln_b": column(L0_attn_ln_b), "u_b": column(uv_b[:E_DIM]),
            "base_b": base_b, "base_b_sw": swap(base_b), "gamma": gamma, "beta": beta, "gamma_sw": swap(gamma),
            "beta_sw": swap(beta), "b1": column(np.asarray(L0_ffn_b1).reshape(-1))}
    local = np.arange(P) % TOK
    w1 = np.asarray(L0_ffn_w1).reshape(EXP, HK, P, DFF).transpose(0, 2, 1, 3).reshape(EXP, P, HK * DFF)
    w2 = np.asarray(L0_ffn_w2).reshape(EXP, DK, P, H).transpose(0, 2, 1, 3).reshape(EXP, P, DK * H)
    arrays = {
        "patchesT": chunks(patches.T),
        "embed_wT": chunks(np.asarray(L0_tok_W).T),
        "uv_wT": chunks(np.asarray(L0_attn_uv_w).T),
        "o_wT": chunks(np.asarray(L0_attn_o_w).T),
        "gate_wT": chunks(np.asarray(L0_ffn_gate_w).T),
        "expert_w": np.concatenate([w1, w2], axis=2),
        "param_cols": np.concatenate([cols[name] for name in COLS], axis=1),
        "param_rows": np.concatenate([np.asarray(L0_attn_o_b), uv_b[E_DIM:2 * E_DIM]]),
        "embed_rows": np.concatenate([
            np.concatenate([np.asarray(L0_tok_pos_emb).reshape(TOK, H), np.asarray(L0_tok_b)[None, :]]),
            np.concatenate([local[None, :] == np.arange(TOK)[:, None], np.ones((1, P), bool)]).astype(np.float32)],
            axis=1),
        "rel_bias": np.asarray(L0_attn_w)[local[:, None] - local[None, :] + BIAS_LEN - 1],
        "expert_b2": np.asarray(L0_ffn_b2).reshape(-1),
        "consts": constant_table(),
    }
    nc = bacc.Bacc("TRN2", target_bir_lowering=False, num_devices=1)
    arrays = {k: np.ascontiguousarray(a) for k, a in arrays.items()}
    ins = [nc.dram_tensor(f"{k}_d", a.shape, mybir.dt.from_np(a.dtype), kind="ExternalInput").ap()
           for k, a in arrays.items()]
    out = nc.dram_tensor("out", [N, H], F32, kind="ExternalOutput").ap()
    build(nc, *ins, out)
    r = run_bass_kernel_spmd(nc, [{f"{k}_d": a for k, a in arrays.items()}], core_ids=[0])
    return r.results[0]["out"].reshape(IMAGES, TOK, H)
```
